# Optimizing a Trainium2 kernel written in Bass

```python
import numpy as np
import jax
import jax.numpy as jnp

def _softmax(x, axis=-1):
    return jax.nn.softmax(x, axis=axis)

def _gelu(x):
    return jax.nn.gelu(x, approximate=True)

def _silu(x):
    return jax.nn.silu(x)

def _sigmoid(x):
    return jax.nn.sigmoid(x)

def _layernorm(x, axis=-1, eps=1e-05):
    m = jnp.mean(x, axis=axis, keepdims=True)
    v = jnp.var(x, axis=axis, keepdims=True)
    return (x - m) / jnp.sqrt(v + eps)

def _scatter_add(tgt, idx, src, axis=0):
    return tgt.at[idx].add(src)

def _segment_sum(src, seg, n):
    return jax.ops.segment_sum(src, seg, n)
kernel_name = 'mk_seq_preln_d1_jaxref_r4_e9fa6a'

def setup_inputs(seed: int=0):
    np.random.seed(seed)
    _w = jnp.asarray

    def _L0_attn_setup():
        import jax, jax.numpy as jnp
        import numpy as np
        DIM = 256
        NUM_HEADS = 16
        HEAD_DIM = DIM // NUM_HEADS
        TAU = 1.0
        LAMBDA_JUMP = 0.6
        LAMBDA_LOCAL = 0.4
        MIN_ENTROPY = 0.5
        WINDOW = 3
        EPS = 1e-10

        def local_diffusion_kernel(seq_len, strength, window=WINDOW):
            i = jnp.arange(seq_len)
            d = i[:, None] - i[None, :]
            k = jnp.where(jnp.abs(d) <= window, jnp.exp(-d.astype(jnp.float32) ** 2 / (2.0 * strength ** 2)), 0.0)
            return k / (k.sum(axis=-1, keepdims=True) + EPS)
        key = jax.random.key(seed)
        ks = jax.random.split(key, 9)
        scale = 0.02
        x = jax.random.normal(ks[0], (2, 512, DIM), dtype=jnp.float32)
        Wq = jax.random.normal(ks[1], (DIM, DIM), dtype=jnp.float32) * scale
        bq = jax.random.normal(ks[2], (DIM,), dtype=jnp.float32) * scale
        Wk = jax.random.normal(ks[3], (DIM, DIM), dtype=jnp.float32) * scale
        bk = jax.random.normal(ks[4], (DIM,), dtype=jnp.float32) * scale
        Wv = jax.random.normal(ks[5], (DIM, DIM), dtype=jnp.float32) * scale
        bv = jax.random.normal(ks[6], (DIM,), dtype=jnp.float32) * scale
        Wo = jax.random.normal(ks[7], (DIM, DIM), dtype=jnp.float32) * scale
        bo = jax.random.normal(ks[8], (DIM,), dtype=jnp.float32) * scale
        return {'x': x, 'Wq': Wq, 'bq': bq, 'Wk': Wk, 'bk': bk, 'Wv': Wv, 'bv': bv, 'Wo': Wo, 'bo': bo}
    _L0_attn_in = _L0_attn_setup()

    def _L0_ffn_setup():
        import jax, jax.numpy as jnp
        import numpy as np
        key = jax.random.key(seed)
        ks = jax.random.split(key, 6)
        B, L, D, E = (4, 512, 256, 4)
        H = 4 * D
        x = jax.random.normal(ks[0], (B, L, D), dtype=jnp.float32)
        rW1 = jax.random.normal(ks[1], (D, 2 * D), dtype=jnp.float32) * (2.0 / D) ** 0.5
        rb1 = jnp.zeros((2 * D,), dtype=jnp.float32)
        rW2 = jax.random.normal(ks[2], (2 * D, E), dtype=jnp.float32) * (2.0 / (2 * D)) ** 0.5
        rb2 = jnp.zeros((E,), dtype=jnp.float32)
        We1 = jax.random.normal(ks[3], (E, D, H), dtype=jnp.float32) * (2.0 / D) ** 0.5
        be1 = jnp.zeros((E, H), dtype=jnp.float32)
        We2 = jax.random.normal(ks[4], (E, H, D), dtype=jnp.float32) * (2.0 / H) ** 0.5
        be2 = jnp.zeros((E, D), dtype=jnp.float32)
        return {'x': x, 'rW1': rW1, 'rb1': rb1, 'rW2': rW2, 'rb2': rb2, 'We1': We1, 'be1': be1, 'We2': We2, 'be2': be2}
    _L0_ffn_in = _L0_ffn_setup()
    _d = {'L0_attn_x': _L0_attn_in['x'], 'L0_attn_Wq': _L0_attn_in['Wq'], 'L0_attn_bq': _L0_attn_in['bq'], 'L0_attn_Wk': _L0_attn_in['Wk'], 'L0_attn_bk': _L0_attn_in['bk'], 'L0_attn_Wv': _L0_attn_in['Wv'], 'L0_attn_bv': _L0_attn_in['bv'], 'L0_attn_Wo': _L0_attn_in['Wo'], 'L0_attn_bo': _L0_attn_in['bo'], 'L0_ffn_rW1': _L0_ffn_in['rW1'], 'L0_ffn_rb1': _L0_ffn_in['rb1'], 'L0_ffn_rW2': _L0_ffn_in['rW2'], 'L0_ffn_rb2': _L0_ffn_in['rb2'], 'L0_ffn_We1': _L0_ffn_in['We1'], 'L0_ffn_be1': _L0_ffn_in['be1'], 'L0_ffn_We2': _L0_ffn_in['We2'], 'L0_ffn_be2': _L0_ffn_in['be2']}
    _x0 = _d['L0_attn_x']
    _d['L0_attn_x'] = jax.random.normal(jax.random.fold_in(jax.random.key(seed), 1), (2, 2048, 256), dtype=_x0.dtype)
    del _x0
    return _d

def reference(L0_attn_x, L0_attn_Wq, L0_attn_bq, L0_attn_Wk, L0_attn_bk, L0_attn_Wv, L0_attn_bv, L0_attn_Wo, L0_attn_bo, L0_ffn_rW1, L0_ffn_rb1, L0_ffn_rW2, L0_ffn_rb2, L0_ffn_We1, L0_ffn_be1, L0_ffn_We2, L0_ffn_be2):

    def _L0_attn_ref(x, Wq, bq, Wk, bk, Wv, bv, Wo, bo):
        import jax, jax.numpy as jnp
        import numpy as np
        DIM = 256
        NUM_HEADS = 16
        HEAD_DIM = DIM // NUM_HEADS
        TAU = 1.0
        LAMBDA_JUMP = 0.6
        LAMBDA_LOCAL = 0.4
        MIN_ENTROPY = 0.5
        WINDOW = 3
        EPS = 1e-10

        def local_diffusion_kernel(seq_len, strength, window=WINDOW):
            i = jnp.arange(seq_len)
            d = i[:, None] - i[None, :]
            k = jnp.where(jnp.abs(d) <= window, jnp.exp(-d.astype(jnp.float32) ** 2 / (2.0 * strength ** 2)), 0.0)
            return k / (k.sum(axis=-1, keepdims=True) + EPS)
        B, S, D = x.shape
        H, hd = (NUM_HEADS, HEAD_DIM)
        Q = (x @ Wq.T + bq).reshape(B, S, H, hd).transpose(0, 2, 1, 3)
        K = (x @ Wk.T + bk).reshape(B, S, H, hd).transpose(0, 2, 1, 3)
        V = (x @ Wv.T + bv).reshape(B, S, H, hd).transpose(0, 2, 1, 3)
        scores = jnp.einsum('bhqd,bhkd->bhqk', Q, K) / (TAU * np.sqrt(hd).astype(np.float32))
        A = jax.nn.softmax(scores, axis=-1)
        entropy = -jnp.sum(A * jnp.log(A + EPS), axis=-1, keepdims=True)
        stable = jax.lax.stop_gradient((entropy >= MIN_ENTROPY).astype(A.dtype))
        A = stable * A + (1.0 - stable) * jax.lax.stop_gradient(A)
        L = local_diffusion_kernel(S, LAMBDA_LOCAL)
        A_stable = LAMBDA_JUMP * A + (1.0 - LAMBDA_JUMP) * L[None, None, :, :]
        out = jnp.einsum('bhqk,bhkd->bhqd', A_stable, V)
        out = out.transpose(0, 2, 1, 3).reshape(B, S, D)
        return out @ Wo.T + bo

    def _L0_ffn_ref(x, rW1, rb1, rW2, rb2, We1, be1, We2, be2):
        import jax, jax.numpy as jnp
        import numpy as np
        E = We1.shape[0]
        top_k = min(2, E)
        rh = jax.nn.gelu(x @ rW1 + rb1, approximate=False)
        router_logits = rh @ rW2 + rb2
        router_probs = jax.nn.softmax(router_logits, axis=-1)
        expert_weights, expert_indices = jax.lax.top_k(router_probs, top_k)
        one_hot = jax.nn.one_hot(expert_indices, E, dtype=x.dtype)
        token_mask = one_hot.sum(axis=2)
        combine_w = (one_hot * expert_weights[..., None]).sum(axis=2)
        out = jnp.zeros_like(x)
        for e in range(E):
            xi = x * token_mask[..., e:e + 1]
            h = jax.nn.gelu(xi @ We1[e] + be1[e], approximate=False)
            yo = h @ We2[e] + be2[e]
            out = out + yo * combine_w[..., e:e + 1]
        return out
    x = L0_attn_x
    x = x + _L0_attn_ref(_layernorm(x, axis=-1), L0_attn_Wq, L0_attn_bq, L0_attn_Wk, L0_attn_bk, L0_attn_Wv, L0_attn_bv, L0_attn_Wo, L0_attn_bo)
    x = x + _L0_ffn_ref(_layernorm(x, axis=-1), L0_ffn_rW1, L0_ffn_rb1, L0_ffn_rW2, L0_ffn_rb2, L0_ffn_We1, L0_ffn_be1, L0_ffn_We2, L0_ffn_be2)
    return x

_drawn_inputs = setup_inputs


def setup_inputs(seed=0):
    import zlib

    import numpy as np

    out = dict(_drawn_inputs(seed))
    spreads = {'L0_ffn_rb1': (0.0, 0.1),
     'L0_ffn_rb2': (0.0, 0.1),
     'L0_ffn_be1': (0.0, 0.1),
     'L0_ffn_be2': (0.0, 0.1)}
    factors = {'L0_attn_Wq': 8.0,
     'L0_attn_bq': 22.08,
     'L0_attn_Wk': 8.0,
     'L0_attn_bk': 64.0,
     'L0_attn_bv': 2.794}
    for name, (base, spread) in spreads.items():
        noise = np.random.default_rng([zlib.crc32(name.encode()), seed]).standard_normal(out[name].shape)
        drawn = base * np.exp(spread * noise) if base else spread * noise
        out[name] = jnp.asarray(drawn.astype(out[name].dtype))
    for name, factor in factors.items():
        out[name] = (out[name] * factor).astype(out[name].dtype)
    return out
```

```python
from contextlib import ExitStack

import numpy as np

import concourse.bass as bass
from concourse import mybir

F32 = mybir.dt.float32
F32R = mybir.dt.float32r
BF16 = mybir.dt.bfloat16
ALU = mybir.AluOpType
ACT = mybir.ActivationFunctionType
AXIS = mybir.AxisListType

P = 128
BATCH, SEQ, DIM = 2, 2048, 256
HEADS = 16
HD = DIM // HEADS
TOKENS = BATCH * SEQ
TILES = TOKENS // P
BT = 4
BLOCK = BT * P
BLOCKS = TOKENS // BLOCK
BPS = SEQ // BLOCK
ST = SEQ // P
KD = DIM // P
NHEADS = BATCH * HEADS
EXPERTS, HIDDEN, RHID = 4, 1024, 512
MH = HIDDEN // P
MR = RHID // P
JUMP, LOCAL_STRENGTH, WINDOW, EPS = 0.6, 0.4, 3, 1e-10
LN_EPS = 1e-5
PIECES = 3
PIECE_RUNS = (3, 2, 1)
STACK = HD * sum(PIECE_RUNS)
SROWS = STACK + PIECES
WIN = P + 2 * WINDOW
BAND = BT * WIN + 2 * WINDOW
LOOK = 20
SHIFT_AT = 13
QUAD = 32
GATE_STEPS = 13


def ds(start, size):
    return bass.ds(start, size)


def twice(engine, pairs, body):
    with engine.Fori(0, pairs - 1) as i:
        body(i, False)
    body(pairs - 1, True)


def wait_apart(engine, count, sem, value, held, held_value):
    if isinstance(value, int):
        engine.wait_ge(sem, value)
    else:
        engine.reg_mov(count, value)
        engine.wait_ge(held, held_value)
        engine.wait_ge(sem, count)


def project(nc, ctx, dram, keep):
    def sb(name, shape, dt=F32):
        return ctx.enter_context(nc.sbuf_tensor(name, shape, dt))

    def sem(name):
        return ctx.enter_context(nc.semaphore(name))

    x_sb, v_sb, ident = keep["x"], keep["v"], keep["ident"]
    w = {n: sb(f"w_{n}", [P, KD, DIM]) for n in "qkv"}
    bias_qk = sb("bias_qk", [P, 2, KD])
    bias_v = sb("bias_v", [P, DIM])
    bias_o = sb("bias_o", [P, DIM])
    half = sb("half", [P, BT])
    stats = [sb(f"stats{u}", [P, BT, 6]) for u in range(2)]
    mv = [sb(f"mv{u}", [P, BT, 2]) for u in range(2)]
    var = [sb(f"var{u}", [P, BT]) for u in range(2)]
    rstd = [sb(f"rstd{u}", [P, BT]) for u in range(2)]
    xn = [sb(f"xn{u}", [P, BT, DIM]) for u in range(2)]
    xnT = [sb(f"xnT{u}", [P, KD, BLOCK]) for u in range(2)]
    pieces = [sb(f"pieces{u}", [P, 2, PIECES, KD, BLOCK], BF16) for u in range(2)]
    rest = [sb(f"rest{c}", [P, BLOCK]) for c in range(2)]
    psum = ctx.enter_context(nc.psum_tensor("psum_project", [P, 8, BLOCK], F32))
    ps_t = [psum[:, 0:2, :], psum[:, 6:8, :]]
    ps_qk = [psum[:, 2, :], psum[:, 3, :]]
    ps_v = [psum[:, 4, :], psum[:, 5, :]]

    const_in, const_set = sem("const_in"), sem("const_set")
    x_in = [sem(f"x_in{u}") for u in range(2)]
    dve_step = sem("dve_step")
    var_ready = [sem(f"var_ready{u}") for u in range(2)]
    rstd_ready = [sem(f"rstd_ready{u}") for u in range(2)]
    xn_ready = [sem(f"xn_ready{u}") for u in range(2)]
    t_ready = [sem(f"t_ready{u}") for u in range(2)]
    xnT_ready = [sem(f"xnT_ready{u}") for u in range(2)]
    qk_ready = [sem(f"qk_ready{c}") for c in range(2)]
    qk_read = [sem(f"qk_read{c}") for c in range(2)]
    piece1 = [sem(f"piece1_{c}") for c in range(2)]
    piece2 = [sem(f"piece2_{c}") for c in range(2)]
    rest2 = [sem(f"rest2_{c}") for c in range(2)]
    piece3 = [sem(f"piece3_{c}") for c in range(2)]
    v_ready = [sem(f"v_ready{c}") for c in range(2)]
    v_read = [sem(f"v_read{c}") for c in range(2)]
    stored = [sem(f"stored{u}") for u in range(2)]
    pairs = BLOCKS // 2
    CONSTS = 9

    block = ctx.enter_context(nc.Block())

    @block.sync
    def _(sp):
        for dst, src in (
            (ident[:], dram["ident"]), (keep["jump"][:], dram["jump"]),
            (w["q"][:], dram["wqT"].rearrange("(k p) n -> p k n", p=P)),
            (w["k"][:], dram["wkT"].rearrange("(k p) n -> p k n", p=P)),
            (w["v"][:], dram["wvT"].rearrange("(k p) n -> p k n", p=P)),
            (bias_qk[:, 0, :], dram["bq"]),
            (bias_qk[:, 1, :], dram["bk"]),
            (bias_v[:], dram["bv"].rearrange("(o f) -> o f", o=1).partition_broadcast(P)),
            (bias_o[:], dram["bo"].rearrange("(o f) -> o f", o=1).partition_broadcast(P)),
        ):
            sp.dma_start(dst, src).then_inc(const_in, 16)
        with sp.Fori(0, pairs) as i:
            for u in range(2):
                t = (2 * i + u) * BT
                sp.wait_ge(x_in[u], 16 * i)
                sp.dma_start(x_sb[:, ds(t, BT), :],
                             dram["x"].rearrange("(n p) f -> p n f", p=P)[:, ds(t, BT), :]).then_inc(x_in[u], 16)
        with sp.Fori(0, pairs) as i:
            for u in range(2):
                blk = 2 * i + u
                for qk in range(2):
                    for m in range(KD):
                        sp.wait_ge(piece3[m], 2 * blk + qk + 1)
                        head = (blk // BPS) * HEADS + m * (HEADS // KD)
                        for c in range(PIECES):
                            dst = dram["qk_pieces"][qk, ds(head, HEADS // KD), c, :, ds((blk % BPS) * BLOCK, BLOCK)]
                            sp.dma_start(dst, pieces[u][:, qk, c, m, :]).then_inc(stored[u], 16)
        for u in range(2):
            sp.wait_ge(stored[u], 16 * 2 * KD * PIECES * pairs)

    @block.gpsimd
    def _(pool):
        nc.gpsimd.memset(half[:], -0.5).then_inc(const_set, 1)
        nc.gpsimd.memset(v_sb[:, :, 0, :], 0.0).then_inc(const_set, 1)
        nc.gpsimd.memset(v_sb[:, :, ST + 1, :], 0.0).then_inc(const_set, 1)
        pool.wait_ge(const_set, 3)

        def rstds(i, last):
            for u in range(2):
                pool.wait_ge(var_ready[u], i + 1)
                nc.gpsimd.tensor_tensor(rstd[u][:], var[u][:], half[:], ALU.pow).then_inc(rstd_ready[u], 1)

        with pool.Fori(0, pairs) as i:
            rstds(i, False)
        pool.wait_ge(const_in, 16 * CONSTS)
        for u in range(2):
            pool.wait_ge(xn_ready[u], pairs)
        nc.gpsimd.tensor_tensor(x_sb[:], x_sb[:], bias_o[:].unsqueeze(1).broadcast_to([P, TILES, DIM]),
                                ALU.add).then_inc(const_set, 1)

    @block.vector
    def _(dve):
        STEPS = 2
        count = dve.alloc_register("project_count")

        def norm(i, u):
            blk = 2 * i + u
            wait_apart(dve, count, x_in[u], 16 * (i + 1), const_in, 16 * CONSTS)
            for t in range(BT):
                last = nc.vector.bn_stats(stats[u][:, t, :], x_sb[:, blk * BT + t, :] if isinstance(blk, int)
                                          else x_sb[:, ds(blk * BT + t, 1), :])
            last.then_inc(dve_step, 1)
            wait_apart(dve, count, dve_step, STEPS * blk + 1, const_in, 16 * CONSTS)
            for t in range(BT):
                last = nc.vector.bn_aggr(mv[u][:, t, :], stats[u][:, t, :])
            last.then_inc(dve_step, 1)
            dve.wait_ge(dve_step, STEPS * blk + 2)
            nc.vector.tensor_scalar_add(var[u][:], mv[u][:, :, 1], LN_EPS).then_inc(var_ready[u], 1)

        def normalise(i, u):
            blk = 2 * i + u
            dve.wait_ge(rstd_ready[u], i + 1)
            dve.wait_ge(t_ready[u], i)
            for t in range(BT):
                last = nc.vector.tensor_scalar(xn[u][:, t, :], x_sb[:, ds(blk * BT + t, 1), :].squeeze(1),
                                               mv[u][:, t, 0:1], rstd[u][:, t:t + 1], ALU.subtract, ALU.mult)
            last.then_inc(xn_ready[u], 1)

        def evacuate(i, u):
            blk = 2 * i + u
            head = (blk // BPS) * HEADS
            for vb in range(2):
                dve.wait_ge(v_ready[vb], blk + 1)
                for t in range(2):
                    kt = 1 + (blk % BPS) * BT + 2 * vb + t
                    last = nc.vector.tensor_tensor(
                        v_sb[:, ds(head, HEADS), ds(kt, 1), :].squeeze(2),
                        ps_v[vb][:, t * DIM:(t + 1) * DIM].rearrange("p (h d) -> p h d", d=HD),
                        bias_v[:].rearrange("p (h d) -> p h d", d=HD), ALU.add)
                last.then_inc(v_read[vb], 1)
            for qk in range(2):
                for m in range(KD):
                    n = 2 * blk + qk
                    dve.wait_ge(piece1[m], n + 1)
                    nc.vector.scalar_tensor_tensor(rest[m][:], ps_qk[m], bias_qk[:, qk, m:m + 1],
                                                   pieces[u][:, qk, 0, m, :], ALU.add, ALU.subtract
                                                   ).then_inc(qk_read[m], 1)
                    dve.wait_ge(qk_read[m], n + 1)
                    nc.vector.tensor_copy(pieces[u][:, qk, 1, m, :], rest[m][:]).then_inc(piece2[m], 1)
                    dve.wait_ge(piece2[m], n + 1)
                    nc.vector.tensor_tensor(pieces[u][:, qk, 2, m, :], rest[m][:], pieces[u][:, qk, 1, m, :],
                                            ALU.subtract).then_inc(piece3[m], 1)

        dve.wait_ge(const_in, 16 * CONSTS)
        norm(0, 0)
        normalise(0, 0)

        def body(i, last):
            norm(i, 1)
            normalise(i, 1)
            evacuate(i, 0)
            if not last:
                norm(i + 1, 0)
                normalise(i + 1, 0)
            evacuate(i, 1)

        twice(dve, pairs, body)

    @block.scalar
    def _(act):
        act.wait_ge(const_in, 16 * CONSTS)

        def copy_T(i, u):
            act.wait_ge(t_ready[u], i + 1)
            nc.scalar.activation(xnT[u][:], ps_t[u], ACT.Copy).then_inc(xnT_ready[u], 1)

        def first_pieces(i, u):
            blk = 2 * i + u
            act.wait_ge(stored[u], 16 * 2 * KD * PIECES * i)
            for qk in range(2):
                for m in range(KD):
                    act.wait_ge(qk_ready[m], 2 * blk + qk + 1)
                    nc.scalar.activation(pieces[u][:, qk, 0, m, :], ps_qk[m], ACT.Identity,
                                         bias=bias_qk[:, qk, m:m + 1]).then_inc(piece1[m], 1)

        copy_T(0, 0)

        def body(i, last):
            copy_T(i, 1)
            first_pieces(i, 0)
            if not last:
                copy_T(i + 1, 0)
            first_pieces(i, 1)

        twice(act, pairs, body)

    @block.tensor
    def _(pe):
        pe.wait_ge(const_in, 16 * CONSTS)

        def transposes(i, u):
            pe.wait_ge(xn_ready[u], i + 1)
            pe.wait_ge(xnT_ready[u], i)
            for k in range(KD):
                for t in range(BT):
                    last = nc.tensor.transpose(ps_t[u][:, k, t * P:(t + 1) * P],
                                               xn[u][:, t, k * P:(k + 1) * P], ident[:])
            last.then_inc(t_ready[u], 1)

        def products(i, u):
            blk = 2 * i + u
            pe.wait_ge(xnT_ready[u], i + 1)
            for vb in range(2):
                pe.wait_ge(v_read[vb], blk)
                for t in range(2):
                    for k in range(KD):
                        last = nc.tensor.matmul(ps_v[vb][:, t * DIM:(t + 1) * DIM],
                                                xnT[u][:, k, (2 * vb + t) * P:(2 * vb + t + 1) * P],
                                                w["v"][:, k, :], start=k == 0, stop=k == KD - 1)
                last.then_inc(v_ready[vb], 1)
            for qk in range(2):
                for m in range(KD):
                    pe.wait_ge(qk_read[m], 2 * blk + qk)
                    for k in range(KD):
                        last = nc.tensor.matmul(ps_qk[m], w["qk"[qk]][:, k, m * P:(m + 1) * P], xnT[u][:, k, :],
                                                start=k == 0, stop=k == KD - 1)
                    last.then_inc(qk_ready[m], 1)

        transposes(0, 0)

        def body(i, last):
            transposes(i, 1)
            products(i, 0)
            if not last:
                transposes(i + 1, 0)
            products(i, 1)

        twice(pe, pairs, body)


def attend(nc, ctx, dram, keep):
    def sb(name, shape, dt=F32):
        return ctx.enter_context(nc.sbuf_tensor(name, shape, dt))

    def sem(name):
        return ctx.enter_context(nc.semaphore(name))

    v_sb, o_sb, ident, ident16 = keep["v"], keep["o"], keep["ident"], keep["ident16"]
    max_q = [sb(f"max_q{u}", [STACK, SEQ], BF16) for u in range(2)]
    max_k = [sb(f"max_k{u}", [STACK, SEQ], BF16) for u in range(2)]
    score_q = [sb(f"score_q{u}", [SROWS, SEQ], BF16) for u in range(2)]
    score_k = [sb(f"score_k{u}", [SROWS, SEQ], BF16) for u in range(2)]
    v_ones = [sb(f"v_ones{u}", [P, ST, QUAD]) for u in range(2)]
    probs = [sb(f"probs{c}", [P, SEQ]) for c in range(2)]
    heads_sb = sb("heads_sb", [P, BLOCK])
    part_max = sb("part_max", [P, ST, BPS])
    neg_max = sb("neg_max", [P, ST])
    shift = sb("shift", [P, PIECES, ST], BF16)
    shift_rest = sb("shift_rest", [P, ST])
    shift_row = sb("shift_row", [PIECES * ST, P], BF16)
    inv_sum = sb("inv_sum", [P, ST])
    psum = ctx.enter_context(nc.psum_tensor("psum_attend", [P, 8, BLOCK], F32))
    ps_s = [psum[:, 0:2, :], psum[:, 2:4, :]]
    ps_m = [psum[:, 4, :], psum[:, 5, :]]
    ps_o = psum[:, 6, :]
    ps_tr = psum[:, 7, :]
    ps_shift = ps_tr[0:PIECES * ST, 0:P // 2].bitcast(BF16)

    ones_set = sem("ones_set")
    max_in = [sem(f"max_in{u}") for u in range(2)]
    score_in = [sem(f"score_in{u}") for u in range(2)]
    shift_in = [sem(f"shift_in{u}") for u in range(2)]
    v_in = [sem(f"v_in{u}") for u in range(2)]
    m_ready = [sem(f"m_ready{c}") for c in range(2)]
    m_read = [sem(f"m_read{c}") for c in range(2)]
    shift_step, shift_ready = sem("shift_step"), sem("shift_ready")
    shift_tr, shift_copied = sem("shift_tr"), sem("shift_copied")
    s_ready = [sem(f"s_ready{c}") for c in range(2)]
    exp_done = [sem(f"exp_done{c}") for c in range(2)]
    pv_done = [sem(f"pv_done{c}") for c in range(2)]
    o_copied, o_tr, o_inv, o_read = sem("o_copied"), sem("o_tr"), sem("o_inv"), sem("o_read")
    pairs = NHEADS // 2
    LOADS = 2 * len(PIECE_RUNS)

    block = ctx.enter_context(nc.Block())

    @block.sync
    def _(sp):
        def load(q_stack, k_stack, n, signal):
            row = 0
            for j, run in enumerate(PIECE_RUNS):
                span = slice(row, row + run * HD)
                sp.dma_start(q_stack[span, :], dram["qk_pieces"][0, ds(n, 1), 0:run, :, :].squeeze(0)
                             ).then_inc(signal, 16)
                sp.dma_start(k_stack[span, :], dram["qk_pieces"][1, ds(n, 1), j:j + 1, :, :].squeeze(0)
                             .broadcast_to([run, HD, SEQ])).then_inc(signal, 16)
                row += run * HD

        def load_shift(m, u):
            sp.wait_ge(shift_copied, m + 1)
            for c in range(PIECES):
                sp.dma_start(score_q[u][STACK + c:STACK + c + 1, :].rearrange("o (t q) -> o t q", q=P),
                             shift_row[c * ST:(c + 1) * ST, :]).then_inc(shift_in[u], 16)

        load(max_q[0], max_k[0], 0, max_in[0])
        load(max_q[1], max_k[1], 1, max_in[1])
        load(score_q[0], score_k[0], 0, score_in[0])
        load(score_q[1], score_k[1], 1, score_in[1])
        load_shift(0, 0)

        def body(i, last):
            for u in range(2):
                n = 2 * i + u
                if not last:
                    sp.wait_ge(m_ready[1], 2 * ST * (n + 1))
                    load(max_q[u], max_k[u], n + 2, max_in[u])
                if not (last and u):
                    load_shift(n + 1, 1 - u)
                if not last:
                    sp.wait_ge(s_ready[1], ST * (n + 1))
                    load(score_q[u], score_k[u], n + 2, score_in[u])

        twice(sp, pairs, body)

    @block.gpsimd
    def _(pool):
        for u in range(2):
            nc.gpsimd.memset(v_ones[u][:], 1.0).then_inc(ones_set, 1)
            pool.wait_ge(ones_set, 2 * u + 1)
            nc.gpsimd.memset(score_k[u][STACK:SROWS, :], 1.0).then_inc(ones_set, 1)
            pool.wait_ge(ones_set, 2 * u + 2)
        nc.gpsimd.tensor_copy(ident16[:], ident[:]).then_inc(ones_set, 1)
        pool.wait_ge(ones_set, 5)

        def stage(n, u):
            nc.gpsimd.tensor_copy(v_ones[u][:, :, 0:HD], v_sb[:, ds(n, 1), 1:ST + 1, :].squeeze(1)
                                  ).then_inc(v_in[u], 1)

        stage(0, 0)
        pool.wait_ge(v_in[0], 1)
        stage(1, 1)
        with pool.Fori(0, pairs - 1) as i:
            for u in range(2):
                n = 2 * i + u
                pool.wait_ge(pv_done[1], ST // 2 * (n + 1))
                pool.wait_ge(v_in[1 - u], i + 1 + u)
                stage(n + 2, u)

    @block.vector
    def _(dve):
        SHIFT_STEPS = 5

        def maxima(g, t):
            for c in range(BPS):
                dve.wait_ge(m_ready[c % 2], 2 * g + c // 2 + 1)
                nc.vector.tensor_reduce(part_max[:, t, c:c + 1], ps_m[c % 2], axis=AXIS.X, op=ALU.max
                                        ).then_inc(m_read[c % 2], 1)

        def split_shift(m):
            for c in range(2):
                dve.wait_ge(m_read[c], 2 * ST * (m + 1))
            base = SHIFT_STEPS * m
            nc.vector.tensor_reduce(neg_max[:], part_max[:], axis=AXIS.X, op=ALU.max, negate=True
                                    ).then_inc(shift_step, 1)
            dve.wait_ge(shift_step, base + 1)
            dve.wait_ge(shift_tr, m)
            nc.vector.tensor_copy(shift[:, 0, :], neg_max[:]).then_inc(shift_step, 1)
            dve.wait_ge(shift_step, base + 2)
            nc.vector.tensor_tensor(shift_rest[:], neg_max[:], shift[:, 0, :], ALU.subtract).then_inc(shift_step, 1)
            dve.wait_ge(shift_step, base + 3)
            nc.vector.tensor_copy(shift[:, 1, :], shift_rest[:]).then_inc(shift_step, 1)
            dve.wait_ge(shift_step, base + 4)
            nc.vector.tensor_tensor(neg_max[:], shift_rest[:], shift[:, 1, :], ALU.subtract).then_inc(shift_step, 1)
            dve.wait_ge(shift_step, base + 5)
            nc.vector.tensor_copy(shift[:, 2, :], neg_max[:]).then_inc(shift_ready, 1)

        def normalise(n):
            tr = ps_tr.rearrange("p (c b e) -> p c b e", c=BT, b=BPS)
            dve.wait_ge(o_tr, n + 1)
            nc.vector.reciprocal(inv_sum[:].rearrange("p (c b) -> p c b", c=BT), tr[:, :, :, HD]
                                 ).then_inc(o_inv, 1)
            dve.wait_ge(o_inv, n + 1)
            out = o_sb[:, ds(n, 1), :, :].squeeze(1).rearrange("p (b c) d -> p c b d", c=BT)
            nc.vector.tensor_tensor(out, tr[:, :, :, 0:HD],
                                    inv_sum[:].rearrange("p (c b) -> p c b", c=BT).unsqueeze(3)
                                    .broadcast_to([P, BT, BPS, HD]), ALU.mult).then_inc(o_read, 1)

        for t in range(ST):
            maxima(t, t)
        split_shift(0)
        for t in range(LOOK - ST):
            maxima(ST + t, t)

        def body(i, last):
            for u in range(2):
                n = 2 * i + u
                for kb in range(ST):
                    ahead = kb + LOOK - ST
                    if not (last and u + ahead // ST > 0):
                        maxima(ST * (n + 1) + ahead, ahead % ST)
                    if ahead == ST - 1 and not (last and u):
                        split_shift(n + 1)
                normalise(n)

        twice(dve, pairs, body)

    @block.scalar
    def _(act):
        def exp(n, kb, c):
            g = ST * n + kb
            act.wait_ge(s_ready[c], g + 1)
            if c == 0:
                act.wait_ge(pv_done[kb % 2], ST // 2 * n + kb // 2)
            nc.scalar.activation(probs[kb % 2][:, c * 2 * BLOCK:(c + 1) * 2 * BLOCK], ps_s[c], ACT.Exp,
                                 scale=float(HD) ** -0.5).then_inc(exp_done[c], 1)

        def copy_shift(m):
            act.wait_ge(shift_tr, m + 1)
            nc.scalar.activation(shift_row[:], ps_shift, ACT.Copy).then_inc(shift_copied, 1)

        copy_shift(0)
        exp(0, 0, 0)

        def body(i, last):
            for u in range(2):
                n = 2 * i + u
                exp(n, 0, 1)
                for kb in range(1, ST):
                    exp(n, kb, 0)
                    if kb == SHIFT_AT and not (last and u):
                        act.wait_ge(shift_in[u], 16 * PIECES * (i + 1))
                        copy_shift(n + 1)
                    exp(n, kb, 1)
                if not (last and u):
                    exp(n + 1, 0, 0)
                act.wait_ge(pv_done[1], ST // 2 * (n + 1))
                act.wait_ge(o_tr, n)
                nc.scalar.activation(heads_sb[:], ps_o, ACT.Copy).then_inc(o_copied, 1)

        twice(act, pairs, body)

    @block.tensor
    def _(pe):
        def maxima(g, t, u, cs):
            for c in cs:
                pe.wait_ge(m_read[c % 2], 2 * g + c // 2)
                last = nc.tensor.matmul(ps_m[c % 2], max_q[u][:, t * P:(t + 1) * P],
                                        max_k[u][:, c * BLOCK:(c + 1) * BLOCK], start=True, stop=True)
                last.then_inc(m_ready[c % 2], 1)

        def scores(g, kb, u, c):
            pe.wait_ge(exp_done[c], g)
            for j in range(2):
                last = nc.tensor.matmul(ps_s[c][:, j, :], score_k[u][:, kb * P:(kb + 1) * P],
                                        score_q[u][:, (2 * c + j) * BLOCK:(2 * c + j + 1) * BLOCK],
                                        start=True, stop=True)
            last.then_inc(s_ready[c], 1)

        def values(n, kb, u):
            pe.wait_ge(exp_done[1], ST * n + kb + 1)
            if kb == 0:
                pe.wait_ge(o_copied, n)
            for j in range(BPS):
                last = nc.tensor.matmul(ps_o[QUAD * j:QUAD * (j + 1), :], v_ones[u][:, kb, :],
                                        probs[kb % 2][:, j * BLOCK:(j + 1) * BLOCK],
                                        start=kb == 0, stop=kb == ST - 1)
            last.then_inc(pv_done[kb % 2], 1)

        count = pe.alloc_register("attend_count")

        def transpose_shift(m):
            if not isinstance(m, int) or m > 0:
                pe.wait_ge(o_read, m - 1)
            wait_apart(pe, count, shift_ready, m + 1, ones_set, 5)
            nc.tensor.transpose(ps_shift, shift[:].rearrange("p c t -> p (c t)"), ident16[:]).then_inc(shift_tr, 1)

        pe.wait_ge(ones_set, 5)
        pe.wait_ge(max_in[0], 16 * LOADS)
        for t in range(ST):
            maxima(t, t, 0, range(BPS))
        pe.wait_ge(max_in[1], 16 * LOADS)
        for t in range(LOOK - ST):
            maxima(ST + t, t, 1, range(BPS))
            if t == 0:
                transpose_shift(0)
        pe.wait_ge(score_in[0], 16 * LOADS)
        pe.wait_ge(shift_in[0], 16 * PIECES)
        for c in range(2):
            scores(0, 0, 0, c)

        def body(i, last):
            for u in range(2):
                n = 2 * i + u
                pe.wait_ge(v_in[u], i + 1)
                for kb in range(ST):
                    ahead = kb + LOOK - ST
                    mu = (u + 1 + ahead // ST) % 2
                    ahead_of_end = last and u + ahead // ST > 0
                    no_next = last and u == 1 and kb == ST - 1
                    if ahead == ST and not ahead_of_end:
                        pe.wait_ge(max_in[mu], 16 * LOADS * (i + 2))
                    if kb == SHIFT_AT and not (last and u):
                        transpose_shift(n + 1)
                    if kb == ST - 1 and not no_next:
                        pe.wait_ge(score_in[1 - u], 16 * LOADS * (i + 1 + u))
                        pe.wait_ge(shift_in[1 - u], 16 * PIECES * (i + 1 + u))
                    for c in range(2):
                        if c == 1 and kb == ST - 1:
                            values(n, kb, u)
                        if not no_next:
                            scores(ST * n + kb + 1, (kb + 1) % ST, u if kb < ST - 1 else 1 - u, c)
                        if not ahead_of_end:
                            maxima(ST * (n + 1) + ahead, ahead % ST, mu, range(2 * c, 2 * c + 2))
                    if kb < ST - 1:
                        values(n, kb, u)
                pe.wait_ge(o_copied, n + 1)
                pe.wait_ge(o_read, n)
                pe.wait_ge(shift_copied, n + (1 if last and u else 2))
                for c in range(BT):
                    last_mm = nc.tensor.transpose(ps_tr[:, c * P:(c + 1) * P], heads_sb[:, c * P:(c + 1) * P],
                                                  ident[:])
                last_mm.then_inc(o_tr, 1)

        twice(pe, pairs, body)


def route(nc, ctx, dram, keep):
    def sb(name, shape, dt=F32):
        return ctx.enter_context(nc.sbuf_tensor(name, shape, dt))

    def sem(name):
        return ctx.enter_context(nc.semaphore(name))

    x_sb, v_sb, o_sb, ident, jump = (keep[n] for n in ("x", "v", "o", "ident", "jump"))
    xT_hi, xT_lo, logits = keep["xT_hi"], keep["xT_lo"], keep["logits"]
    w_o = sb("w_o", [P, KD, DIM])
    band = sb("band", [P, BAND])
    w_r1_hi = sb("w_r1_hi", [P, KD, RHID], F32R)
    w_r1_lo = sb("w_r1_lo", [P, KD, RHID], F32R)
    w_r2 = sb("w_r2", [P, MR, QUAD])
    b_r1 = sb("b_r1", [P, MR])
    half = sb("half_route", [P, BT])
    o_st = sb("o_st", [P, BT, DIM])
    v_st = sb("v_st", [P, BT, DIM])
    v_halo = sb("v_halo", [P, DIM])
    attnT = sb("attnT", [P, KD, BLOCK])
    stats = sb("stats_route", [P, BT, 6])
    mv = sb("mv_route", [P, BT, 2])
    var = sb("var_route", [P, BT])
    rstd = sb("rstd_route", [P, BT])
    xn = sb("xn_route", [P, BT, DIM])
    rh = sb("rh", [P, MR, BLOCK])
    w_r1 = rh[:, 0:KD, :]
    logitsT = sb("logitsT", [P, BLOCK])
    psum = ctx.enter_context(nc.psum_tensor("psum_route", [P, 8, BLOCK], F32))
    ps_a = [psum[:, 0, :], psum[:, 1, :]]
    ps_w = psum[:, 2:4, :]
    ps_t = psum[:, 4:6, :]
    ps_r = [psum[:, 6, :], psum[:, 7, :]]

    const_in, half_set = sem("route_const_in"), sem("half_set")
    w_hi, w_lo = sem("w_r1_hi_set"), sem("w_r1_lo_set")
    band_in, staged = sem("band_in"), sem("staged")
    a_ready = [sem(f"a_ready{m}") for m in range(KD)]
    a_copied = [sem(f"a_copied{m}") for m in range(KD)]
    o_ready, residual = sem("o_ready"), sem("residual")
    stat_step, var_ready, rstd_ready = sem("stat_step"), sem("route_var"), sem("route_rstd")
    xn_ready, t_ready, hi_ready, lo_ready = (sem(n) for n in ("route_xn", "route_t", "hi_ready", "lo_ready"))
    r_ready = [sem(f"r_ready{m}") for m in range(MR)]
    rh_ready = [sem(f"rh_ready{m}") for m in range(MR)]
    lg_ready, lg_copied, lg_tr, lg_read = (sem(n) for n in ("lg_ready", "lg_copied", "lg_tr", "lg_read"))
    CONSTS = 4

    block = ctx.enter_context(nc.Block())

    def steps(engine, first, second):
        first(0)
        with engine.Fori(0, BLOCKS - 1) as i:
            first(i + 1)
            second(i)
        second(BLOCKS - 1)

    @block.sync
    def _(sp):
        for dst, src in ((w_r1, dram["rW1"].rearrange("(k p) n -> p k n", p=P)),
                         (w_o[:], dram["woT"].rearrange("(k p) n -> p k n", p=P)),
                         (w_r2[:], dram["rW2"].rearrange("(k p) n -> p k n", p=P)),
                         (b_r1[:], dram["rb1"])):
            sp.dma_start(dst, src).then_inc(const_in, 16)
        with sp.Fori(0, BLOCKS) as i:
            sp.wait_ge(a_ready[KD - 1], i)
            sp.dma_start(band[:], dram["band"][ds(i % BPS, 1)].squeeze(0)).then_inc(band_in, 16)

    @block.gpsimd
    def _(pool):
        nc.gpsimd.memset(half[:], -0.5).then_inc(half_set, 1)
        pool.wait_ge(half_set, 1)
        with pool.Fori(0, BLOCKS) as i:
            pool.wait_ge(var_ready, i + 1)
            nc.gpsimd.tensor_tensor(rstd[:], var[:], half[:], ALU.pow).then_inc(rstd_ready, 1)

    @block.scalar
    def _(act):
        def stage(i):
            heads, kt = (i // BPS) * HEADS, (i % BPS) * BT
            act.wait_ge(a_ready[KD - 1], i)
            def tiles(src, at, n):
                return src[:, ds(heads, HEADS), ds(at, n), :].rearrange("p h t d -> p t h d")
            def to(dst):
                return dst[:].rearrange("p t (h d) -> p t h d", d=HD)
            nc.scalar.activation(to(o_st), tiles(o_sb, kt, BT), ACT.Copy)
            nc.scalar.activation(to(v_st), tiles(v_sb, kt + 1, BT), ACT.Copy)
            for p0, p1, at in ((0, 64, kt + BT + 1), (64, 96, kt + BT + 1), (96, P, kt)):
                last = nc.scalar.activation(v_halo[p0:p1, :].rearrange("p (h d) -> p h d", d=HD),
                                            v_sb[p0:p1, ds(heads, HEADS), ds(at, 1), :].squeeze(2), ACT.Copy)
            last.then_inc(staged, 1)

        def first(i):
            for m in range(KD):
                act.wait_ge(a_ready[m], i + 1)
                if m == 0:
                    act.wait_ge(o_ready, i)
                nc.scalar.activation(attnT[:, m, :], ps_a[m], ACT.Copy).then_inc(a_copied[m], 1)

        def second(i):
            act.wait_ge(t_ready, i + 1)
            nc.scalar.activation(xT_hi[:, :, ds(i * BLOCK, BLOCK)], ps_t, ACT.Copy).then_inc(hi_ready, 1)
            for m in range(MR):
                act.wait_ge(r_ready[m], i + 1)
                nc.scalar.activation(rh[:, m, :], ps_r[m % 2], ACT.Gelu, bias=b_r1[:, m:m + 1]
                                     ).then_inc(rh_ready[m], 1)
            act.wait_ge(lg_ready, i + 1)
            nc.scalar.activation(logitsT[:], ps_r[0], ACT.Copy).then_inc(lg_copied, 1)

        act.wait_ge(const_in, 16 * CONSTS)
        nc.scalar.activation(w_r1_hi[:], w_r1, ACT.Copy).then_inc(w_hi, 1)
        act.wait_ge(w_lo, 1)
        stage(0)
        first(0)
        with act.Fori(0, BLOCKS - 1) as i:
            stage(i + 1)
            first(i + 1)
            second(i)
        second(BLOCKS - 1)

    @block.vector
    def _(dve):
        count = dve.alloc_register("route_count")
        dve.wait_ge(w_hi, 1)
        nc.vector.tensor_tensor(w_r1_lo[:], w_r1, w_r1_hi[:].bitcast(F32), ALU.subtract).then_inc(w_lo, 1)

        def first(i):
            tiles = ds(i * BT, BT)
            dve.wait_ge(o_ready, i + 1)
            nc.vector.tensor_tensor(x_sb[:, tiles, :].rearrange("p t f -> p (t f)"),
                                    ps_w.rearrange("p b f -> p (b f)"),
                                    x_sb[:, tiles, :].rearrange("p t f -> p (t f)"), ALU.add).then_inc(residual, 1)
            wait_apart(dve, count, residual, i + 1, w_lo, 1)
            for t in range(BT):
                last = nc.vector.bn_stats(stats[:, t, :], x_sb[:, ds(i * BT + t, 1), :].squeeze(1))
            last.then_inc(stat_step, 1)
            wait_apart(dve, count, stat_step, 2 * i + 1, w_lo, 1)
            for t in range(BT):
                last = nc.vector.bn_aggr(mv[:, t, :], stats[:, t, :])
            last.then_inc(stat_step, 1)
            dve.wait_ge(stat_step, 2 * i + 2)
            nc.vector.tensor_scalar_add(var[:], mv[:, :, 1], LN_EPS).then_inc(var_ready, 1)
            dve.wait_ge(rstd_ready, i + 1)
            dve.wait_ge(t_ready, i)
            for t in range(BT):
                last = nc.vector.tensor_scalar(xn[:, t, :], x_sb[:, ds(i * BT + t, 1), :].squeeze(1),
                                               mv[:, t, 0:1], rstd[:, t:t + 1], ALU.subtract, ALU.mult)
            last.then_inc(xn_ready, 1)

        def second(i):
            cols = ds(i * BLOCK, BLOCK)
            dve.wait_ge(hi_ready, i + 1)
            nc.vector.tensor_tensor(xT_lo[:, :, cols], ps_t, xT_hi[:, :, cols].bitcast(F32), ALU.subtract
                                    ).then_inc(lo_ready, 1)
            dve.wait_ge(lg_tr, i + 1)
            nc.vector.tensor_reduce(logits[:, ds(i * BT, BT), :],
                                    ps_r[1].rearrange("p (c j e) -> p c e j", c=BT, j=MR)[:, :, 0:EXPERTS, :],
                                    axis=AXIS.X, op=ALU.add).then_inc(lg_read, 1)

        first(0)
        with dve.Fori(0, BLOCKS - 1) as i:
            first(i + 1)
            second(i)
        second(BLOCKS - 1)

    @block.tensor
    def _(pe):
        pe.wait_ge(const_in, 16 * CONSTS)
        pe.wait_ge(w_lo, 1)

        def first(i):
            pe.wait_ge(band_in, 16 * (i + 1))
            pe.wait_ge(staged, i + 1)
            for m in range(KD):
                pe.wait_ge(a_copied[m], i)
                feats = slice(m * P, (m + 1) * P)
                for t in range(BT):
                    nc.tensor.matmul(ps_a[m][:, t * P:(t + 1) * P], o_st[:, t, feats], jump[:],
                                     start=t == 0, stop=False)
                for t in range(BT):
                    q0, q1 = max(0, t * P - WINDOW), min(BLOCK, (t + 1) * P + WINDOW)
                    c0 = t * WIN + q0 - (t * P - WINDOW)
                    nc.tensor.matmul(ps_a[m][:, q0:q1], v_st[:, t, feats], band[:, c0:c0 + q1 - q0],
                                     start=False, stop=False)
                for q0, c0 in ((0, BT * WIN), (BLOCK - WINDOW, BT * WIN + WINDOW)):
                    last = nc.tensor.matmul(ps_a[m][:, q0:q0 + WINDOW], v_halo[:, feats], band[:, c0:c0 + WINDOW],
                                            start=False, stop=q0 > 0)
                last.then_inc(a_ready[m], 1)
            for m in range(KD):
                pe.wait_ge(a_copied[m], i + 1)
            pe.wait_ge(residual, i)
            for t in range(BT):
                for k in range(KD):
                    last = nc.tensor.matmul(ps_w[:, t // 2, (t % 2) * DIM:(t % 2 + 1) * DIM],
                                            attnT[:, k, t * P:(t + 1) * P], w_o[:, k, :],
                                            start=k == 0, stop=k == KD - 1)
            last.then_inc(o_ready, 1)

        def second(i):
            pe.wait_ge(xn_ready, i + 1)
            pe.wait_ge(lo_ready, i)
            for k in range(KD):
                for t in range(BT):
                    last = nc.tensor.transpose(ps_t[:, k, t * P:(t + 1) * P], xn[:, t, k * P:(k + 1) * P], ident[:])
            last.then_inc(t_ready, 1)
            pe.wait_ge(lo_ready, i + 1)
            cols = ds(i * BLOCK, BLOCK)
            for m in range(MR):
                if m == 0:
                    pe.wait_ge(lg_copied, i)
                elif m == 1:
                    pe.wait_ge(lg_read, i)
                else:
                    pe.wait_ge(rh_ready[m - 2], i + 1)
                feats = slice(m * P, (m + 1) * P)
                terms = [(w, xs, k) for w, xs in ((w_r1_hi, xT_hi), (w_r1_hi, xT_lo), (w_r1_lo, xT_hi))
                         for k in range(KD)]
                for n, (w, xs, k) in enumerate(terms):
                    last = nc.tensor.matmul(ps_r[m % 2], w[:, k, feats], xs[:, k, cols],
                                            start=n == 0, stop=n == len(terms) - 1)
                last.then_inc(r_ready[m], 1)
            for m in range(MR):
                pe.wait_ge(rh_ready[m], i + 1)
            for m in range(MR):
                last = nc.tensor.matmul(ps_r[0][m * QUAD:(m + 1) * QUAD, :], w_r2[:, m, :], rh[:, m, :],
                                        start=True, stop=True)
            last.then_inc(lg_ready, 1)
            pe.wait_ge(lg_copied, i + 1)
            for c in range(BT):
                last = nc.tensor.transpose(ps_r[1][:, c * P:(c + 1) * P], logitsT[:, c * P:(c + 1) * P], ident[:])
            last.then_inc(lg_tr, 1)

        steps(pe, first, second)


def experts(nc, ctx, dram, keep):
    def sb(name, shape, dt=F32):
        return ctx.enter_context(nc.sbuf_tensor(name, shape, dt))

    def sem(name):
        return ctx.enter_context(nc.semaphore(name))

    x_sb, xT_hi, xT_lo, logits = (keep[n] for n in ("x", "xT_hi", "xT_lo", "logits"))
    raw1 = sb("raw1", [P, KD, HIDDEN])
    raw2 = sb("raw2", [P, MH, DIM])
    w1 = [(sb(f"w1_hi{u}", [P, KD, HIDDEN], F32R), sb(f"w1_lo{u}", [P, KD, HIDDEN], F32R)) for u in range(2)]
    w2 = [(sb(f"w2_hi{u}", [P, MH, DIM], F32R), sb(f"w2_lo{u}", [P, MH, DIM], F32R)) for u in range(2)]
    b1 = sb("b1", [P, EXPERTS, MH])
    b2 = sb("b2", [P, EXPERTS, DIM])
    b_r2 = sb("b_r2", [P, EXPERTS])
    before = sb("before", [P, 2, EXPERTS, EXPERTS])
    h = [sb(f"h{c}", [P, BLOCK]) for c in range(2)]
    h_hi = [sb(f"h_hi{c}", [P, BLOCK], F32R) for c in range(4)]
    h_lo = [sb(f"h_lo{c}", [P, BLOCK], F32R) for c in range(4)]
    NT = [P, TILES]
    top = sb("top", NT)
    prob = sb("prob", [P, TILES, EXPERTS])
    cmp = [sb(f"cmp{c}", [P, TILES, EXPERTS, EXPERTS]) for c in range(1)]
    cmp.append(h[0][:].rearrange("p (t e j) -> p t e j", e=EXPERTS, j=EXPERTS))
    rank = sb("rank", [P, TILES, EXPERTS])
    gate = sb("gate", [P, TILES, EXPERTS])
    psum = ctx.enter_context(nc.psum_tensor("psum_experts", [P, 8, BLOCK], F32))
    ps_h = [psum[:, c, :] for c in range(2)]
    ps_y = [psum[:, 2 + t, 0:DIM] for t in range(BT)]

    const_in = sem("expert_const_in")
    raw_in, hi_set, lo_set = sem("raw_in"), sem("weights_hi"), sem("weights_lo")
    gate_step, shifted, exp_ready = sem("gate_step"), sem("shifted"), sem("exp_ready")
    h_ready = [sem(f"h_ready{c}") for c in range(2)]
    gelu_done = [sem(f"gelu_done{c}") for c in range(2)]
    h_hi_ready = sem("h_hi_ready")
    h_lo_ready = [sem(f"h_lo_ready{c}") for c in range(2)]
    h_used = [sem(f"h_used{c}") for c in range(4)]
    y_ready = [sem(f"y_ready{t}") for t in range(BT - 1)]
    y_read = [sem(f"y_read{t}") for t in range(BT)]
    acc_done, out_stored = sem("acc_done"), sem("out_stored")
    CONSTS = 4

    block = ctx.enter_context(nc.Block())

    @block.sync
    def _(sp):
        for e in range(EXPERTS):
            sp.wait_ge(lo_set, 2 * e)
            sp.dma_start(raw1[:], dram["We1"][e].rearrange("(k p) n -> p k n", p=P)).then_inc(raw_in, 16)
            sp.dma_start(raw2[:], dram["We2"][e].rearrange("(k p) n -> p k n", p=P)).then_inc(raw_in, 16)
            if e == 0:
                for dst, src in ((b1[:], dram["be1"]), (b2[:], dram["be2"].rearrange("(o e) f -> o e f", o=1)
                                                        .partition_broadcast(P)),
                                 (b_r2[:], dram["rb2"].rearrange("(o e) -> o e", o=1).partition_broadcast(P)),
                                 (before[:], dram["before"].rearrange("(o c) e j -> o c e j", o=1)
                                  .partition_broadcast(P))):
                    sp.dma_start(dst, src).then_inc(const_in, 16)
        with sp.Fori(0, BLOCKS) as i:
            sp.wait_ge(acc_done, (EXPERTS - 1) * BLOCKS + i + 1)
            sp.dma_start(dram["out"].rearrange("(n p) f -> p n f", p=P)[:, ds(i * BT, BT), :],
                         x_sb[:, ds(i * BT, BT), :]).then_inc(out_stored, 16)
        sp.wait_ge(out_stored, 16 * BLOCKS)

    @block.gpsimd
    def _(pool):
        for e in range(1, EXPERTS):
            pool.wait_ge(raw_in, 32 * (e + 1))
            if e >= 2:
                pool.wait_ge(h_used[3], 2 * BLOCKS * (e - 1))
            for n, (raw, w) in enumerate(((raw1, w1), (raw2, w2))):
                nc.gpsimd.tensor_copy(w[e % 2][0][:], raw[:]).then_inc(hi_set, 1)
                pool.wait_ge(hi_set, 2 * e + n + 1)
                nc.gpsimd.tensor_tensor(w[e % 2][1][:], raw[:], w[e % 2][0][:].bitcast(F32), ALU.subtract
                                        ).then_inc(lo_set, 1)
                pool.wait_ge(lo_set, 2 * e + n + 1)

    @block.scalar
    def _(act):
        act.wait_ge(shifted, 1)
        nc.scalar.activation(prob[:], prob[:], ACT.Exp).then_inc(exp_ready, 1)
        act.wait_ge(raw_in, 32)
        for n, (raw, w) in enumerate(((raw1, w1), (raw2, w2))):
            nc.scalar.activation(w[0][0][:], raw[:], ACT.Copy).then_inc(hi_set, 1)
        act.wait_ge(const_in, 16 * CONSTS)
        act.wait_ge(gate_step, GATE_STEPS)
        for e in range(EXPERTS):
            with act.Fori(0, BLOCKS) as b:
                n = e * BLOCKS + b
                for m in range(MH):
                    act.wait_ge(h_ready[m % 2], MH // 2 * n + m // 2 + 1)
                    act.wait_ge(h_lo_ready[m % 2], MH // 2 * n + m // 2)
                    nc.scalar.activation(h[m % 2][:], ps_h[m % 2], ACT.Gelu, bias=b1[:, e, m:m + 1]
                                         ).then_inc(gelu_done[m % 2], 1)

    @block.vector
    def _(dve):
        done = [0]

        def gate_op(instruction):
            instruction.then_inc(gate_step, 1)
            done[0] += 1
            dve.wait_ge(gate_step, done[0])

        per_tile = [P, TILES, EXPERTS]
        pairs = [P, TILES, EXPERTS, EXPERTS]
        dve.wait_ge(const_in, 16 * CONSTS)
        gate_op(nc.vector.tensor_tensor(logits[:], logits[:], b_r2[:].unsqueeze(1).broadcast_to(per_tile), ALU.add))
        gate_op(nc.vector.tensor_reduce(top[:], logits[:], axis=AXIS.X, op=ALU.max))
        nc.vector.tensor_tensor(prob[:], logits[:], top[:].unsqueeze(2).broadcast_to(per_tile), ALU.subtract
                                ).then_inc(shifted, 1)
        dve.wait_ge(exp_ready, 1)
        gate_op(nc.vector.tensor_reduce(top[:], prob[:], axis=AXIS.X, op=ALU.add))
        gate_op(nc.vector.reciprocal(top[:], top[:]))
        gate_op(nc.vector.tensor_tensor(prob[:], prob[:], top[:].unsqueeze(2).broadcast_to(per_tile), ALU.mult))
        p_j, p_e = prob[:].unsqueeze(2).broadcast_to(pairs), prob[:].unsqueeze(3).broadcast_to(pairs)
        for c, op in enumerate((ALU.is_gt, ALU.is_ge)):
            scratch = cmp[c] if c else cmp[c][:]
            gate_op(nc.vector.tensor_tensor(scratch, p_j, p_e, op))
            gate_op(nc.vector.tensor_tensor(scratch, scratch, before[:, c].unsqueeze(1).broadcast_to(pairs),
                                            ALU.mult))
        gate_op(nc.vector.tensor_tensor(cmp[1], cmp[1], cmp[0][:], ALU.add))
        gate_op(nc.vector.tensor_reduce(rank[:], cmp[1], axis=AXIS.X, op=ALU.add))
        gate_op(nc.vector.tensor_scalar(rank[:], rank[:], 1.5, None, ALU.is_lt))
        gate_op(nc.vector.tensor_tensor(gate[:], prob[:], rank[:], ALU.mult))
        assert done[0] == GATE_STEPS
        for n, (raw, w) in enumerate(((raw1, w1), (raw2, w2))):
            dve.wait_ge(hi_set, n + 1)
            nc.vector.tensor_tensor(w[0][1][:], raw[:], w[0][0][:].bitcast(F32), ALU.subtract).then_inc(lo_set, 1)

        def halves(n, m):
            s = MH * n + m
            dve.wait_ge(gelu_done[m % 2], MH // 2 * n + m // 2 + 1)
            dve.wait_ge(h_used[m % 4], MH // 4 * n + m // 4)
            nc.vector.tensor_copy(h_hi[m % 4][:], h[m % 2][:]).then_inc(h_hi_ready, 1)
            dve.wait_ge(h_hi_ready, s + 1)
            nc.vector.tensor_tensor(h_lo[m % 4][:], h[m % 2][:], h_hi[m % 4][:].bitcast(F32), ALU.subtract
                                    ).then_inc(h_lo_ready[m % 2], 1)

        def accumulate(e, b):
            n = e * BLOCKS + b
            dve.wait_ge(acc_done, n)
            for t in range(BT):
                acc, g = x_sb[:, ds(b * BT + t, 1), :].squeeze(1), gate[:, ds(b * BT + t, 1), e]
                if t < BT - 1:
                    dve.wait_ge(y_ready[t], n + 1)
                else:
                    dve.wait_ge(h_used[3], 2 * (n + 1))
                nc.vector.scalar_tensor_tensor(acc, ps_y[t], g, acc, ALU.mult, ALU.add).then_inc(y_read[t], 1)
            for t in range(BT):
                acc, g = x_sb[:, ds(b * BT + t, 1), :].squeeze(1), gate[:, ds(b * BT + t, 1), e]
                dve.wait_ge(y_read[t], n + 1)
                last = nc.vector.scalar_tensor_tensor(acc, b2[:, e, :], g, acc, ALU.mult, ALU.add)
            last.then_inc(acc_done, 1)

        halves(0, 0)
        for e in range(EXPERTS):
            def body(b, last):
                n = e * BLOCKS + b
                for m in range(1, MH):
                    halves(n, m)
                if not (last and e == EXPERTS - 1):
                    halves(n + 1, 0)
                accumulate(e, b)

            twice(dve, BLOCKS, body)

    @block.tensor
    def _(pe):
        def hidden(e, b, m):
            n = e * BLOCKS + b
            pe.wait_ge(gelu_done[m % 2], MH // 2 * n + m // 2)
            feats, cols = slice(m * P, (m + 1) * P), ds(b * BLOCK, BLOCK)
            hi, lo = w1[e % 2]
            terms = [(w, xs, k) for w, xs in ((hi, xT_hi), (hi, xT_lo), (lo, xT_hi)) for k in range(KD)]
            for j, (w, xs, k) in enumerate(terms):
                last = nc.tensor.matmul(ps_h[m % 2], w[:, k, feats], xs[:, k, cols],
                                        start=j == 0, stop=j == len(terms) - 1)
            last.then_inc(h_ready[m % 2], 1)

        def output(e, b, m):
            n = e * BLOCKS + b
            hi, lo = w2[e % 2]
            pe.wait_ge(h_lo_ready[m % 2], MH // 2 * n + m // 2 + 1)
            for t in range(BT):
                toks = slice(t * P, (t + 1) * P)
                if m == 0:
                    pe.wait_ge(y_read[t], n)
                terms = ((h_hi, hi), (h_hi, lo), (h_lo, hi))
                for j, (hs, w) in enumerate(terms):
                    last = nc.tensor.matmul(ps_y[t], hs[m % 4][:, toks], w[:, m, :],
                                            start=m == 0 and j == 0, stop=m == MH - 1 and j == 2)
                if t == BT - 1:
                    last.then_inc(h_used[m % 4], 1)
                elif m == MH - 1:
                    last.then_inc(y_ready[t], 1)

        pe.wait_ge(lo_set, 1)
        hidden(0, 0, 0)
        pe.wait_ge(lo_set, 2)
        for e in range(EXPERTS):
            def body(b, last):
                for m in range(MH):
                    if m < MH - 1:
                        hidden(e, b, m + 1)
                    elif not last:
                        hidden(e, b + 1, 0)
                    elif e < EXPERTS - 1:
                        pe.wait_ge(lo_set, 2 * (e + 2))
                        hidden(e + 1, 0, 0)
                    output(e, b, m)

            twice(pe, BLOCKS, body)


def program(nc, dram):
    with ExitStack() as whole:
        def sb(name, shape, dt=F32):
            return whole.enter_context(nc.sbuf_tensor(name, shape, dt))

        keep = {
            "x": sb("x_sb", [P, TILES, DIM]), "ident": sb("ident_sb", [P, P]), "jump": sb("jump_sb", [P, P]),
            "ident16": sb("ident16", [P, P], BF16), "logits": sb("logits", [P, TILES, EXPERTS]),
        }
        dram["qk_pieces"] = nc.dram_tensor("qk_pieces", (2, NHEADS, PIECES, HD, SEQ), BF16, kind="Internal").ap()
        with ExitStack() as tokens:
            for n, tiles in (("v", ST + 2), ("o", ST)):
                keep[n] = tokens.enter_context(nc.sbuf_tensor(f"{n}_sb", [P, NHEADS, tiles, HD], F32))
            for stage in (project, attend):
                with ExitStack() as ctx:
                    stage(nc, ctx, dram, keep)
            for n in ("xT_hi", "xT_lo"):
                keep[n] = whole.enter_context(nc.sbuf_tensor(n, [P, KD, TOKENS], F32R, side="right"))
            with ExitStack() as ctx:
                route(nc, ctx, dram, keep)
        with ExitStack() as ctx:
            experts(nc, ctx, dram, keep)


def local_band():
    q, t = np.arange(SEQ)[:, None], np.arange(SEQ)[None, :]
    d = (q - t).astype(np.float32)
    k = np.where(np.abs(d) <= WINDOW, np.exp(-d ** 2 / np.float32(2.0 * LOCAL_STRENGTH ** 2)), np.float32(0))
    k = (np.float32(1.0 - JUMP) * (k / (k.sum(-1, keepdims=True, dtype=np.float32) + np.float32(EPS)))).astype(np.float32)
    padded = np.zeros((SEQ + 2 * P, SEQ + 2 * P), np.float32)
    padded[P:-P, P:-P] = k
    band = np.zeros((BPS, P, BAND), np.float32)
    for j in range(BPS):
        start = P + j * BLOCK
        for t in range(BT):
            key = start + t * P
            band[j, :, t * WIN:(t + 1) * WIN] = padded[key - WINDOW:key + P + WINDOW, key:key + P].T
        halo = band[j, :, BT * WIN:]
        halo[96:, 0:WINDOW] = padded[start:start + WINDOW, start - P:start].T[96:]
        end = start + BLOCK
        halo[:96, WINDOW:] = padded[end - WINDOW:end, end:end + P].T[:96]
    return band


def kernel(**inputs):
    import concourse.bacc as bacc
    from concourse.bass_utils import run_bass_kernel_spmd

    a = {n.split("_", 2)[2]: np.asarray(v) for n, v in inputs.items() if n.startswith("L0_attn_")}
    f = {n.split("_", 2)[2]: np.asarray(v) for n, v in inputs.items() if n.startswith("L0_ffn_")}
    eye = np.eye(P, dtype=np.float32)
    j, e = np.arange(EXPERTS)[None, :], np.arange(EXPERTS)[:, None]
    w_r2 = np.zeros((RHID, QUAD), np.float32)
    w_r2[:, :EXPERTS] = f["rW2"]

    def columns(v):
        return v.reshape(-1, P).T

    arrays = {
        "x": a["x"].reshape(TOKENS, DIM),
        "wqT": a["Wq"].T, "wkT": a["Wk"].T, "wvT": a["Wv"].T, "woT": a["Wo"].T,
        "bq": columns(a["bq"]), "bk": columns(a["bk"]), "bv": a["bv"], "bo": a["bo"],
        "rW1": f["rW1"], "rb1": columns(f["rb1"]), "rW2": w_r2, "rb2": f["rb2"],
        "We1": f["We1"], "be1": f["be1"].reshape(EXPERTS, MH, P).transpose(2, 0, 1), "We2": f["We2"], "be2": f["be2"],
        "ident": eye, "jump": np.float32(JUMP) * eye, "band": local_band(),
        "before": np.stack([j > e, j < e]).astype(np.float32),
    }
    nc = bacc.Bacc("TRN2", target_bir_lowering=False, num_devices=1)
    arrays = {n: np.ascontiguousarray(v) for n, v in arrays.items()}
    dram = {n: nc.dram_tensor(f"in_{n}", v.shape, mybir.dt.from_np(v.dtype), kind="ExternalInput").ap()
            for n, v in arrays.items()}
    dram["out"] = nc.dram_tensor("out", (TOKENS, DIM), F32, kind="ExternalOutput").ap()
    program(nc, dram)
    r = run_bass_kernel_spmd(nc, [{f"in_{n}": v for n, v in arrays.items()}], core_ids=[0])
    return r.results[0]["out"].reshape(BATCH, SEQ, DIM)
```

```python
from contextlib import ExitStack

import numpy as np

import concourse.bass as bass
from concourse import mybir

F32 = mybir.dt.float32
F32R = mybir.dt.float32r
BF16 = mybir.dt.bfloat16
ALU = mybir.AluOpType
ACT = mybir.ActivationFunctionType
AXIS = mybir.AxisListType

P = 128
BATCH, SEQ, DIM = 2, 2048, 256
HEADS = 16
HD = DIM // HEADS
TOKENS = BATCH * SEQ
TILES = TOKENS // P
BT = 4
BLOCK = BT * P
BLOCKS = TOKENS // BLOCK
BPS = SEQ // BLOCK
ST = SEQ // P
KD = DIM // P
NHEADS = BATCH * HEADS
EXPERTS, HIDDEN, RHID = 4, 1024, 512
MH = HIDDEN // P
MR = RHID // P
JUMP, LOCAL_STRENGTH, WINDOW, EPS = 0.6, 0.4, 3, 1e-10
LN_EPS = 1e-5
PIECES = 3
PIECE_RUNS = (3, 2, 1)
STACK = HD * sum(PIECE_RUNS)
SROWS = STACK + PIECES
WIN = P + 2 * WINDOW
BAND = BT * WIN + 2 * WINDOW
LOOK = 20
SHIFT_AT = 13
QUAD = 32
GATE_STEPS = 13


def ds(start, size):
    return bass.ds(start, size)


def twice(engine, pairs, body):
    with engine.Fori(0, pairs - 1) as i:
        body(i, False)
    body(pairs - 1, True)


def wait_apart(engine, count, sem, value, held, held_value):
    if isinstance(value, int):
        engine.wait_ge(sem, value)
    else:
        engine.reg_mov(count, value)
        engine.wait_ge(held, held_value)
        engine.wait_ge(sem, count)


def project(nc, ctx, dram, keep):
    def sb(name, shape, dt=F32):
        return ctx.enter_context(nc.sbuf_tensor(name, shape, dt))

    def sem(name):
        return ctx.enter_context(nc.semaphore(name))

    x_sb, v_sb, ident = keep["x"], keep["v"], keep["ident"]
    w = {n: sb(f"w_{n}", [P, KD, DIM]) for n in "qkv"}
    bias_qk = sb("bias_qk", [P, 2, KD])
    bias_v = sb("bias_v", [P, DIM])
    bias_o = sb("bias_o", [P, DIM])
    half = sb("half", [P, BT])
    stats = [sb(f"stats{u}", [P, BT, 6]) for u in range(2)]
    mv = [sb(f"mv{u}", [P, BT, 2]) for u in range(2)]
    var = [sb(f"var{u}", [P, BT]) for u in range(2)]
    rstd = [sb(f"rstd{u}", [P, BT]) for u in range(2)]
    xn = [sb(f"xn{u}", [P, BT, DIM]) for u in range(2)]
    xnT = [sb(f"xnT{u}", [P, KD, BLOCK]) for u in range(2)]
    pieces = [sb(f"pieces{u}", [P, 2, PIECES, KD, BLOCK], BF16) for u in range(2)]
    rest = [sb(f"rest{c}", [P, BLOCK]) for c in range(2)]
    psum = ctx.enter_context(nc.psum_tensor("psum_project", [P, 8, BLOCK], F32))
    ps_t = [psum[:, 0:2, :], psum[:, 6:8, :]]
    ps_qk = [psum[:, 2, :], psum[:, 3, :]]
    ps_v = [psum[:, 4, :], psum[:, 5, :]]

    const_in, const_set = sem("const_in"), sem("const_set")
    x_in = [sem(f"x_in{u}") for u in range(2)]
    dve_step = sem("dve_step")
    var_ready = [sem(f"var_ready{u}") for u in range(2)]
    rstd_ready = [sem(f"rstd_ready{u}") for u in range(2)]
    xn_ready = [sem(f"xn_ready{u}") for u in range(2)]
    t_ready = [sem(f"t_ready{u}") for u in range(2)]
    xnT_ready = [sem(f"xnT_ready{u}") for u in range(2)]
    qk_ready = [sem(f"qk_ready{c}") for c in range(2)]
    qk_read = [sem(f"qk_read{c}") for c in range(2)]
    piece1 = [sem(f"piece1_{c}") for c in range(2)]
    piece2 = [sem(f"piece2_{c}") for c in range(2)]
    rest2 = [sem(f"rest2_{c}") for c in range(2)]
    piece3 = [sem(f"piece3_{c}") for c in range(2)]
    v_ready = [sem(f"v_ready{c}") for c in range(2)]
    v_read = [sem(f"v_read{c}") for c in range(2)]
    stored = [sem(f"stored{u}") for u in range(2)]
    pairs = BLOCKS // 2
    CONSTS = 9

    block = ctx.enter_context(nc.Block())

    @block.sync
    def _(sp):
        for dst, src in (
            (ident[:], dram["ident"]), (keep["jump"][:], dram["jump"]),
            (w["q"][:], dram["wqT"].rearrange("(k p) n -> p k n", p=P)),
            (w["k"][:], dram["wkT"].rearrange("(k p) n -> p k n", p=P)),
            (w["v"][:], dram["wvT"].rearrange("(k p) n -> p k n", p=P)),
            (bias_qk[:, 0, :], dram["bq"]),
            (bias_qk[:, 1, :], dram["bk"]),
            (bias_v[:], dram["bv"].rearrange("(o f) -> o f", o=1).partition_broadcast(P)),
            (bias_o[:], dram["bo"].rearrange("(o f) -> o f", o=1).partition_broadcast(P)),
        ):
            sp.dma_start(dst, src).then_inc(const_in, 16)
        with sp.Fori(0, pairs) as i:
            for u in range(2):
                t = (2 * i + u) * BT
                sp.wait_ge(x_in[u], 16 * i)
                sp.dma_start(x_sb[:, ds(t, BT), :],
                             dram["x"].rearrange("(n p) f -> p n f", p=P)[:, ds(t, BT), :]).then_inc(x_in[u], 16)
        with sp.Fori(0, pairs) as i:
            for u in range(2):
                blk = 2 * i + u
                for qk in range(2):
                    for m in range(KD):
                        sp.wait_ge(piece3[m], 2 * blk + qk + 1)
                        head = (blk // BPS) * HEADS + m * (HEADS // KD)
                        for c in range(PIECES):
                            dst = dram["qk_pieces"][qk, ds(head, HEADS // KD), c, :, ds((blk % BPS) * BLOCK, BLOCK)]
                            sp.dma_start(dst, pieces[u][:, qk, c, m, :]).then_inc(stored[u], 16)
        for u in range(2):
            sp.wait_ge(stored[u], 16 * 2 * KD * PIECES * pairs)

    @block.gpsimd
    def _(pool):
        nc.gpsimd.memset(half[:], -0.5).then_inc(const_set, 1)
        nc.gpsimd.memset(v_sb[:, :, 0, :], 0.0).then_inc(const_set, 1)
        nc.gpsimd.memset(v_sb[:, :, ST + 1, :], 0.0).then_inc(const_set, 1)
        pool.wait_ge(const_set, 3)

        def rstds(i, last):
            for u in range(2):
                pool.wait_ge(var_ready[u], i + 1)
                nc.gpsimd.tensor_tensor(rstd[u][:], var[u][:], half[:], ALU.pow).then_inc(rstd_ready[u], 1)

        with pool.Fori(0, pairs) as i:
            rstds(i, False)
        pool.wait_ge(const_in, 16 * CONSTS)
        for u in range(2):
            pool.wait_ge(xn_ready[u], pairs)
        nc.gpsimd.tensor_tensor(x_sb[:], x_sb[:], bias_o[:].unsqueeze(1).broadcast_to([P, TILES, DIM]),
                                ALU.add).then_inc(const_set, 1)

    @block.vector
    def _(dve):
        STEPS = 2
        count = dve.alloc_register("project_count")

        def norm(i, u):
            blk = 2 * i + u
            wait_apart(dve, count, x_in[u], 16 * (i + 1), const_in, 16 * CONSTS)
            for t in range(BT):
                last = nc.vector.bn_stats(stats[u][:, t, :], x_sb[:, blk * BT + t, :] if isinstance(blk, int)
                                          else x_sb[:, ds(blk * BT + t, 1), :])
            last.then_inc(dve_step, 1)
            wait_apart(dve, count, dve_step, STEPS * blk + 1, const_in, 16 * CONSTS)
            for t in range(BT):
                last = nc.vector.bn_aggr(mv[u][:, t, :], stats[u][:, t, :])
            last.then_inc(dve_step, 1)
            dve.wait_ge(dve_step, STEPS * blk + 2)
            nc.vector.tensor_scalar_add(var[u][:], mv[u][:, :, 1], LN_EPS).then_inc(var_ready[u], 1)

        def normalise(i, u):
            blk = 2 * i + u
            dve.wait_ge(rstd_ready[u], i + 1)
            dve.wait_ge(t_ready[u], i)
            for t in range(BT):
                last = nc.vector.tensor_scalar(xn[u][:, t, :], x_sb[:, ds(blk * BT + t, 1), :].squeeze(1),
                                               mv[u][:, t, 0:1], rstd[u][:, t:t + 1], ALU.subtract, ALU.mult)
            last.then_inc(xn_ready[u], 1)

        def evacuate(i, u):
            blk = 2 * i + u
            head = (blk // BPS) * HEADS
            for vb in range(2):
                dve.wait_ge(v_ready[vb], blk + 1)
                for t in range(2):
                    kt = 1 + (blk % BPS) * BT + 2 * vb + t
                    last = nc.vector.tensor_tensor(
                        v_sb[:, ds(head, HEADS), ds(kt, 1), :].squeeze(2),
                        ps_v[vb][:, t * DIM:(t + 1) * DIM].rearrange("p (h d) -> p h d", d=HD),
                        bias_v[:].rearrange("p (h d) -> p h d", d=HD), ALU.add)
                last.then_inc(v_read[vb], 1)
            for qk in range(2):
                for m in range(KD):
                    n = 2 * blk + qk
                    dve.wait_ge(piece1[m], n + 1)
                    nc.vector.scalar_tensor_tensor(rest[m][:], ps_qk[m], bias_qk[:, qk, m:m + 1],
                                                   pieces[u][:, qk, 0, m, :], ALU.add, ALU.subtract
                                                   ).then_inc(qk_read[m], 1)
                    dve.wait_ge(qk_read[m], n + 1)
                    nc.vector.tensor_copy(pieces[u][:, qk, 1, m, :], rest[m][:]).then_inc(piece2[m], 1)
                    dve.wait_ge(piece2[m], n + 1)
                    nc.vector.tensor_tensor(pieces[u][:, qk, 2, m, :], rest[m][:], pieces[u][:, qk, 1, m, :],
                                            ALU.subtract).then_inc(piece3[m], 1)

        dve.wait_ge(const_in, 16 * CONSTS)
        norm(0, 0)
        normalise(0, 0)

        def body(i, last):
            norm(i, 1)
            normalise(i, 1)
            evacuate(i, 0)
            if not last:
                norm(i + 1, 0)
                normalise(i + 1, 0)
            evacuate(i, 1)

        twice(dve, pairs, body)

    @block.scalar
    def _(act):
        act.wait_ge(const_in, 16 * CONSTS)

        def copy_T(i, u):
            act.wait_ge(t_ready[u], i + 1)
            nc.scalar.activation(xnT[u][:], ps_t[u], ACT.Copy).then_inc(xnT_ready[u], 1)

        def first_pieces(i, u):
            blk = 2 * i + u
            act.wait_ge(stored[u], 16 * 2 * KD * PIECES * i)
            for qk in range(2):
                for m in range(KD):
                    act.wait_ge(qk_ready[m], 2 * blk + qk + 1)
                    nc.scalar.activation(pieces[u][:, qk, 0, m, :], ps_qk[m], ACT.Identity,
                                         bias=bias_qk[:, qk, m:m + 1]).then_inc(piece1[m], 1)

        copy_T(0, 0)

        def body(i, last):
            copy_T(i, 1)
            first_pieces(i, 0)
            if not last:
                copy_T(i + 1, 0)
            first_pieces(i, 1)

        twice(act, pairs, body)

    @block.tensor
    def _(pe):
        pe.wait_ge(const_in, 16 * CONSTS)

        def transposes(i, u):
            pe.wait_ge(xn_ready[u], i + 1)
            pe.wait_ge(xnT_ready[u], i)
            for k in range(KD):
                for t in range(BT):
                    last = nc.tensor.transpose(ps_t[u][:, k, t * P:(t + 1) * P],
                                               xn[u][:, t, k * P:(k + 1) * P], ident[:])
            last.then_inc(t_ready[u], 1)

        def products(i, u):
            blk = 2 * i + u
            pe.wait_ge(xnT_ready[u], i + 1)
            for vb in range(2):
                pe.wait_ge(v_read[vb], blk)
                for t in range(2):
                    for k in range(KD):
                        last = nc.tensor.matmul(ps_v[vb][:, t * DIM:(t + 1) * DIM],
                                                xnT[u][:, k, (2 * vb + t) * P:(2 * vb + t + 1) * P],
                                                w["v"][:, k, :], start=k == 0, stop=k == KD - 1)
                last.then_inc(v_ready[vb], 1)
            for qk in range(2):
                for m in range(KD):
                    pe.wait_ge(qk_read[m], 2 * blk + qk)
                    for k in range(KD):
                        last = nc.tensor.matmul(ps_qk[m], w["qk"[qk]][:, k, m * P:(m + 1) * P], xnT[u][:, k, :],
                                                start=k == 0, stop=k == KD - 1)
                    last.then_inc(qk_ready[m], 1)

        transposes(0, 0)

        def body(i, last):
            transposes(i, 1)
            products(i, 0)
            if not last:
                transposes(i + 1, 0)
            products(i, 1)

        twice(pe, pairs, body)


def attend(nc, ctx, dram, keep):
    def sb(name, shape, dt=F32):
        return ctx.enter_context(nc.sbuf_tensor(name, shape, dt))

    def sem(name):
        return ctx.enter_context(nc.semaphore(name))

    v_sb, o_sb, ident, ident16 = keep["v"], keep["o"], keep["ident"], keep["ident16"]
    max_q = [sb(f"max_q{u}", [STACK, SEQ], BF16) for u in range(2)]
    max_k = [sb(f"max_k{u}", [STACK, SEQ], BF16) for u in range(2)]
    score_q = [sb(f"score_q{u}", [SROWS, SEQ], BF16) for u in range(2)]
    score_k = [sb(f"score_k{u}", [SROWS, SEQ], BF16) for u in range(2)]
    v_ones = [sb(f"v_ones{u}", [P, ST, QUAD]) for u in range(2)]
    probs = [sb(f"probs{c}", [P, SEQ]) for c in range(2)]
    heads_sb = sb("heads_sb", [P, BLOCK])
    heads_tok = sb("heads_tok", [P, BLOCK])
    part_max = sb("part_max", [P, ST, 2])
    neg_max = sb("neg_max", [P, ST])
    shift = sb("shift", [P, PIECES, ST], BF16)
    shift_rest = sb("shift_rest", [P, ST])
    shift_row = sb("shift_row", [PIECES * ST, P], BF16)
    inv_sum = sb("inv_sum", [P, ST])
    psum = ctx.enter_context(nc.psum_tensor("psum_attend", [P, 8, BLOCK], F32))
    ps_s = [psum[:, c, :] for c in range(3)]
    ps_o = psum[:, 3, :]
    ps_m = [psum[:, 4:6, :], psum[:, 6:8, :]]
    ps_tr = psum[:, 7, :]
    ps_shift = ps_tr[0:PIECES * ST, 0:P // 2].bitcast(BF16)
    CH = BPS

    ones_set = sem("ones_set")
    max_in = [sem(f"max_in{u}") for u in range(2)]
    score_in = [sem(f"score_in{u}") for u in range(2)]
    shift_in = [sem(f"shift_in{u}") for u in range(2)]
    v_in = sem("v_in")
    m_ready, m_read = sem("m_ready"), sem("m_read")
    shift_step, shift_ready = sem("shift_step"), sem("shift_ready")
    shift_tr, shift_copied = sem("shift_tr"), sem("shift_copied")
    s_ready, exp_done = sem("s_ready"), sem("exp_done")
    pv_done = sem("pv_done")
    o_copied = sem("o_copied")
    o_tr, tok_copied = sem("o_tr"), sem("tok_copied")
    inv_ready = sem("inv_ready")
    tok_used = sem("tok_used")
    pairs = NHEADS // 2
    LOADS = 2 * len(PIECE_RUNS)
    PV_OPEN = 2
    POOL_SET = 6

    block = ctx.enter_context(nc.Block())

    @block.sync
    def _(sp):
        def load(q_stack, k_stack, n, signal):
            row = 0
            for j, run in enumerate(PIECE_RUNS):
                span = slice(row, row + run * HD)
                sp.dma_start(q_stack[span, :], dram["qk_pieces"][0, ds(n, 1), 0:run, :, :].squeeze(0)
                             ).then_inc(signal, 16)
                sp.dma_start(k_stack[span, :], dram["qk_pieces"][1, ds(n, 1), j:j + 1, :, :].squeeze(0)
                             .broadcast_to([run, HD, SEQ])).then_inc(signal, 16)
                row += run * HD

        def load_shift(m, u):
            sp.wait_ge(shift_copied, m + 1)
            for c in range(PIECES):
                sp.dma_start(score_q[u][STACK + c:STACK + c + 1, :].rearrange("o (t q) -> o t q", q=P),
                             shift_row[c * ST:(c + 1) * ST, :]).then_inc(shift_in[u], 16)

        load(max_q[0], max_k[0], 0, max_in[0])
        load(score_q[0], score_k[0], 0, score_in[0])
        load(max_q[1], max_k[1], 1, max_in[1])
        load(score_q[1], score_k[1], 1, score_in[1])
        load_shift(0, 0)

        def body(i, last):
            for u in range(2):
                n = 2 * i + u
                if not last:
                    sp.wait_ge(m_ready, 2 * ST * (n + 1))
                    load(max_q[u], max_k[u], n + 2, max_in[u])
                if not (last and u):
                    load_shift(n + 1, 1 - u)
                if not last:
                    sp.wait_ge(s_ready, CH * ST * (n + 1))
                    load(score_q[u], score_k[u], n + 2, score_in[u])

        twice(sp, pairs, body)

    @block.gpsimd
    def _(pool):
        for u in range(2):
            nc.gpsimd.memset(v_ones[u][:], 1.0).then_inc(ones_set, 1)
            pool.wait_ge(ones_set, 2 * u + 1)
            nc.gpsimd.memset(score_k[u][STACK:SROWS, :], 1.0).then_inc(ones_set, 1)
            pool.wait_ge(ones_set, 2 * u + 2)
        nc.gpsimd.tensor_copy(ident16[:], ident[:]).then_inc(ones_set, 1)
        pool.wait_ge(ones_set, 5)
        nc.gpsimd.memset(heads_sb[:], 1.0).then_inc(o_copied, 1)
        pool.wait_ge(o_copied, 1)

        def stage(n, u):
            nc.gpsimd.tensor_copy(v_ones[u][:, :, 0:HD], v_sb[:, ds(n, 1), 1:ST + 1, :].squeeze(1)
                                  ).then_inc(v_in, 1)

        stage(0, 0)
        pool.wait_ge(v_in, 1)
        stage(1, 1)
        with pool.Fori(0, pairs - 1) as i:
            for u in range(2):
                n = 2 * i + u
                pool.wait_ge(pv_done, ST * (n + 1) + PV_OPEN)
                pool.wait_ge(v_in, n + 2)
                stage(n + 2, u)

    @block.vector
    def _(dve):
        def maxima(g, t):
            for p in range(2):
                dve.wait_ge(m_ready, 2 * g + p + 1)
                nc.vector.tensor_reduce(part_max[:, t, p:p + 1], ps_m[p].rearrange("q b f -> q (b f)"),
                                        axis=AXIS.X, op=ALU.max).then_inc(m_read, 1)

        def split_shift(m):
            dve.wait_ge(m_read, 2 * ST * (m + 1))
            base = 5 * m
            nc.vector.tensor_reduce(neg_max[:], part_max[:], axis=AXIS.X, op=ALU.max, negate=True
                                    ).then_inc(shift_step, 1)
            dve.wait_ge(shift_step, base + 1)
            if not isinstance(m, int) or m > 0:
                dve.wait_ge(shift_tr, m)
            nc.vector.tensor_copy(shift[:, 0, :], neg_max[:]).then_inc(shift_step, 1)
            dve.wait_ge(shift_step, base + 2)
            nc.vector.tensor_tensor(shift_rest[:], neg_max[:], shift[:, 0, :], ALU.subtract).then_inc(shift_step, 1)
            dve.wait_ge(shift_step, base + 3)
            nc.vector.tensor_copy(shift[:, 1, :], shift_rest[:]).then_inc(shift_step, 1)
            dve.wait_ge(shift_step, base + 4)
            nc.vector.tensor_tensor(neg_max[:], shift_rest[:], shift[:, 1, :], ALU.subtract).then_inc(shift_step, 1)
            dve.wait_ge(shift_step, base + 5)
            nc.vector.tensor_copy(shift[:, 2, :], neg_max[:]).then_inc(shift_ready, 1)

        def normalise(n):
            tok = heads_tok[:].rearrange("p (c b e) -> p c b e", c=BT, b=BPS)
            inv = inv_sum[:].rearrange("p (c b) -> p c b", c=BT)
            dve.wait_ge(tok_copied, n + 1)
            nc.vector.reciprocal(inv, tok[:, :, :, HD]).then_inc(inv_ready, 1)
            dve.wait_ge(inv_ready, n + 1)
            out = o_sb[:, ds(n, 1), :, :].squeeze(1).rearrange("p (b c) d -> p c b d", c=BT)
            nc.vector.tensor_tensor(out, tok[:, :, :, 0:HD], inv.unsqueeze(3).broadcast_to([P, BT, BPS, HD]),
                                    ALU.mult).then_inc(tok_used, 1)

        for t in range(ST):
            maxima(t, t)
        split_shift(0)
        for t in range(LOOK - ST):
            maxima(ST + t, t)

        def body(i, last):
            for u in range(2):
                n = 2 * i + u
                for kb in range(ST):
                    ahead = kb + LOOK - ST
                    if not (last and u + ahead // ST > 0):
                        maxima(ST * (n + 1) + ahead, ahead % ST)
                    if kb == 1:
                        normalise(n)
                    if ahead == ST - 1 and not (last and u):
                        split_shift(n + 1)

        twice(dve, pairs, body)
        normalise(NHEADS)

    @block.scalar
    def _(act):
        act.sem_inc(pv_done, PV_OPEN)
        act.sem_inc(tok_used, 1)

        def exp(n, kb, c):
            j = CH * kb + c
            act.wait_ge(s_ready, CH * ST * n + j + 1)
            if c == 0:
                act.wait_ge(pv_done, ST * n + kb - 1 + PV_OPEN)
            nc.scalar.activation(probs[kb % 2][:, c * BLOCK:(c + 1) * BLOCK], ps_s[j % 3], ACT.Exp,
                                 scale=float(HD) ** -0.5).then_inc(exp_done, 1)

        def copy_shift(m):
            act.wait_ge(shift_tr, m + 1)
            nc.scalar.activation(shift_row[:], ps_shift, ACT.Copy).then_inc(shift_copied, 1)

        def copy_tok(n):
            act.wait_ge(tok_used, n + 1)
            act.wait_ge(o_tr, n + 1)
            nc.scalar.activation(heads_tok[:], ps_tr, ACT.Copy).then_inc(tok_copied, 1)

        copy_shift(0)
        for c in range(CH):
            exp(0, 0, c)

        def body(i, last):
            for u in range(2):
                n = 2 * i + u
                for kb in range(1, ST):
                    exp(n, kb, 0)
                    if kb == 1:
                        copy_tok(n)
                    if kb == SHIFT_AT + 1 and not (last and u):
                        act.wait_ge(shift_in[u], 16 * PIECES * (i + 1))
                        copy_shift(n + 1)
                    for c in range(1, CH):
                        exp(n, kb, c)
                if not (last and u):
                    for c in range(CH):
                        exp(n + 1, 0, c)
                act.wait_ge(o_tr, n + 1)
                act.wait_ge(pv_done, ST * (n + 1) + PV_OPEN)
                nc.scalar.activation(heads_sb[:], ps_o, ACT.Copy).then_inc(o_copied, 1)

        twice(act, pairs, body)
        copy_tok(NHEADS)

    @block.tensor
    def _(pe):
        count = pe.alloc_register("attend_count")

        def maxima(g, t, u, p):
            if not isinstance(g, int) or g > 0:
                pe.wait_ge(m_read, 2 * g + p - 1)
            for j in range(2):
                c = 2 * p + j
                last = nc.tensor.matmul(ps_m[p][:, j, :], max_q[u][:, t * P:(t + 1) * P],
                                        max_k[u][:, c * BLOCK:(c + 1) * BLOCK], start=True, stop=True)
            last.then_inc(m_ready, 1)

        def scores(n, kb, u, c):
            j = CH * kb + c
            g = CH * ST * n + j
            used = g if j == 0 else g - 2
            if not isinstance(used, int) or used > 0:
                pe.wait_ge(exp_done, used)
            nc.tensor.matmul(ps_s[j % 3], score_k[u][:, kb * P:(kb + 1) * P],
                             score_q[u][:, c * BLOCK:(c + 1) * BLOCK], start=True, stop=True).then_inc(s_ready, 1)

        def values(n, kb, u):
            pe.wait_ge(exp_done, CH * (ST * n + kb + 1))
            if kb == 0:
                pe.wait_ge(o_copied, n + 1)
            for j in range(BPS):
                last = nc.tensor.matmul(ps_o[QUAD * j:QUAD * (j + 1), :], v_ones[u][:, kb, :],
                                        probs[kb % 2][:, j * BLOCK:(j + 1) * BLOCK],
                                        start=kb == 0, stop=kb == ST - 1)
            last.then_inc(pv_done, 1)

        def transpose_shift(m):
            wait_apart(pe, count, shift_ready, m + 1, ones_set, POOL_SET - 1)
            nc.tensor.transpose(ps_shift, shift[:].rearrange("p c t -> p (c t)"), ident16[:]).then_inc(shift_tr, 1)

        def transpose_heads(n):
            pe.wait_ge(o_copied, n + 1)
            for c in range(BT):
                last = nc.tensor.transpose(ps_tr[:, c * P:(c + 1) * P], heads_sb[:, c * P:(c + 1) * P], ident[:])
            last.then_inc(o_tr, 1)

        pe.wait_ge(ones_set, POOL_SET - 1)
        pe.wait_ge(max_in[0], 16 * LOADS)
        for t in range(ST):
            for p in range(2):
                maxima(t, t, 0, p)
        pe.wait_ge(max_in[1], 16 * LOADS)
        for t in range(LOOK - ST):
            for p in range(2):
                if (t, p) == (1, 1):
                    pe.wait_ge(m_read, 2 * (ST + 1))
                    transpose_shift(0)
                    pe.wait_ge(shift_copied, 1)
                maxima(ST + t, t, 1, p)
        pe.wait_ge(score_in[0], 16 * LOADS)
        pe.wait_ge(shift_in[0], 16 * PIECES)
        for c in range(CH):
            scores(0, 0, 0, c)

        def body(i, last):
            for u in range(2):
                n = 2 * i + u
                pe.wait_ge(v_in, n + 1)
                for kb in range(ST):
                    ahead = kb + LOOK - ST
                    g, mu = ST * (n + 1) + ahead, (u + 1 + ahead // ST) % 2
                    more_maxima = not (last and u + ahead // ST > 0)
                    more_scores = not (last and u == 1 and kb == ST - 1)
                    nxt = (n, kb + 1, u) if kb < ST - 1 else (n + 1, 0, 1 - u)
                    if ahead == ST and more_maxima:
                        pe.wait_ge(max_in[mu], 16 * LOADS * (i + 2))
                    if kb == ST - 1 and more_scores:
                        pe.wait_ge(score_in[1 - u], 16 * LOADS * (i + 1 + u))
                        pe.wait_ge(shift_in[1 - u], 16 * PIECES * (i + 1 + u))
                    if more_scores:
                        scores(*nxt, 0)
                    if more_maxima:
                        maxima(g, ahead % ST, mu, 0)
                    if kb == 0:
                        pe.wait_ge(m_read, 2 * g if more_maxima else 2 * ST * NHEADS)
                        transpose_heads(n)
                    if kb == SHIFT_AT and not (last and u):
                        pe.wait_ge(m_read, 2 * g if more_maxima else 2 * ST * NHEADS)
                        transpose_shift(n + 1)
                    if more_scores:
                        for c in range(1, CH):
                            scores(*nxt, c)
                    if more_maxima:
                        if kb == 0:
                            pe.wait_ge(tok_copied, n + 1)
                        if kb == SHIFT_AT:
                            pe.wait_ge(shift_copied, n + 2)
                        maxima(g, ahead % ST, mu, 1)
                    values(n, kb, u)

        twice(pe, pairs, body)
        pe.wait_ge(tok_copied, NHEADS)
        transpose_heads(NHEADS)


def route(nc, ctx, dram, keep):
    def sb(name, shape, dt=F32):
        return ctx.enter_context(nc.sbuf_tensor(name, shape, dt))

    def sem(name):
        return ctx.enter_context(nc.semaphore(name))

    x_sb, v_sb, o_sb, ident, jump = (keep[n] for n in ("x", "v", "o", "ident", "jump"))
    xT_hi, xT_lo, logits = keep["xT_hi"], keep["xT_lo"], keep["logits"]
    w_o = sb("w_o", [P, KD, DIM])
    band = sb("band", [P, BAND])
    w_r1_hi = sb("w_r1_hi", [P, KD, RHID], F32R)
    w_r1_lo = sb("w_r1_lo", [P, KD, RHID], F32R)
    w_r2 = sb("w_r2", [P, MR, QUAD])
    b_r1 = sb("b_r1", [P, MR])
    half = sb("half_route", [P, BT])
    o_st = sb("o_st", [P, BT, DIM])
    v_st = sb("v_st", [P, BT, DIM])
    v_halo = sb("v_halo", [P, DIM])
    attnT = sb("attnT", [P, KD, BLOCK])
    stats = sb("stats_route", [P, BT, 6])
    mv = sb("mv_route", [P, BT, 2])
    var = sb("var_route", [P, BT])
    rstd = sb("rstd_route", [P, BT])
    xn = sb("xn_route", [P, BT, DIM])
    rh = sb("rh", [P, MR, BLOCK])
    w_r1 = rh[:, 0:KD, :]
    logitsT = sb("logitsT", [P, BLOCK])
    psum = ctx.enter_context(nc.psum_tensor("psum_route", [P, 8, BLOCK], F32))
    ps_a = [psum[:, 0, :], psum[:, 1, :]]
    ps_w = psum[:, 2:4, :]
    ps_t = psum[:, 4:6, :]
    ps_r = [psum[:, 6, :], psum[:, 7, :]]

    const_in, half_set = sem("route_const_in"), sem("half_set")
    w_hi, w_lo = sem("w_r1_hi_set"), sem("w_r1_lo_set")
    band_in, staged = sem("band_in"), sem("staged")
    a_ready = [sem(f"a_ready{m}") for m in range(KD)]
    a_copied = [sem(f"a_copied{m}") for m in range(KD)]
    o_ready, residual = sem("o_ready"), sem("residual")
    stat_step, var_ready, rstd_ready = sem("stat_step"), sem("route_var"), sem("route_rstd")
    xn_ready, t_ready, hi_ready, lo_ready = (sem(n) for n in ("route_xn", "route_t", "hi_ready", "lo_ready"))
    r_ready = [sem(f"r_ready{m}") for m in range(MR)]
    rh_ready = [sem(f"rh_ready{m}") for m in range(MR)]
    lg_ready, lg_copied, lg_tr, lg_read = (sem(n) for n in ("lg_ready", "lg_copied", "lg_tr", "lg_read"))
    CONSTS = 4

    block = ctx.enter_context(nc.Block())

    def steps(engine, first, second):
        first(0)
        with engine.Fori(0, BLOCKS - 1) as i:
            first(i + 1)
            second(i)
        second(BLOCKS - 1)

    @block.sync
    def _(sp):
        for dst, src in ((w_r1, dram["rW1"].rearrange("(k p) n -> p k n", p=P)),
                         (w_o[:], dram["woT"].rearrange("(k p) n -> p k n", p=P)),
                         (w_r2[:], dram["rW2"].rearrange("(k p) n -> p k n", p=P)),
                         (b_r1[:], dram["rb1"])):
            sp.dma_start(dst, src).then_inc(const_in, 16)
        with sp.Fori(0, BLOCKS) as i:
            sp.wait_ge(a_ready[KD - 1], i)
            sp.dma_start(band[:], dram["band"][ds(i % BPS, 1)].squeeze(0)).then_inc(band_in, 16)

    @block.gpsimd
    def _(pool):
        nc.gpsimd.memset(half[:], -0.5).then_inc(half_set, 1)
        pool.wait_ge(half_set, 1)
        with pool.Fori(0, BLOCKS) as i:
            pool.wait_ge(var_ready, i + 1)
            nc.gpsimd.tensor_tensor(rstd[:], var[:], half[:], ALU.pow).then_inc(rstd_ready, 1)

    @block.scalar
    def _(act):
        def stage(i):
            heads, kt = (i // BPS) * HEADS, (i % BPS) * BT
            act.wait_ge(a_ready[KD - 1], i)
            def tiles(src, at, n):
                return src[:, ds(heads, HEADS), ds(at, n), :].rearrange("p h t d -> p t h d")
            def to(dst):
                return dst[:].rearrange("p t (h d) -> p t h d", d=HD)
            nc.scalar.activation(to(o_st), tiles(o_sb[:, 1:NHEADS + 1], kt, BT), ACT.Copy)
            nc.scalar.activation(to(v_st), tiles(v_sb, kt + 1, BT), ACT.Copy)
            for p0, p1, at in ((0, 64, kt + BT + 1), (64, 96, kt + BT + 1), (96, P, kt)):
                last = nc.scalar.activation(v_halo[p0:p1, :].rearrange("p (h d) -> p h d", d=HD),
                                            v_sb[p0:p1, ds(heads, HEADS), ds(at, 1), :].squeeze(2), ACT.Copy)
            last.then_inc(staged, 1)

        def first(i):
            for m in range(KD):
                act.wait_ge(a_ready[m], i + 1)
                if m == 0:
                    act.wait_ge(o_ready, i)
                nc.scalar.activation(attnT[:, m, :], ps_a[m], ACT.Copy).then_inc(a_copied[m], 1)

        def second(i):
            act.wait_ge(t_ready, i + 1)
            nc.scalar.activation(xT_hi[:, :, ds(i * BLOCK, BLOCK)], ps_t, ACT.Copy).then_inc(hi_ready, 1)
            for m in range(MR):
                act.wait_ge(r_ready[m], i + 1)
                nc.scalar.activation(rh[:, m, :], ps_r[m % 2], ACT.Gelu, bias=b_r1[:, m:m + 1]
                                     ).then_inc(rh_ready[m], 1)
            act.wait_ge(lg_ready, i + 1)
            nc.scalar.activation(logitsT[:], ps_r[0], ACT.Copy).then_inc(lg_copied, 1)

        act.wait_ge(const_in, 16 * CONSTS)
        nc.scalar.activation(w_r1_hi[:], w_r1, ACT.Copy).then_inc(w_hi, 1)
        act.wait_ge(w_lo, 1)
        stage(0)
        first(0)
        with act.Fori(0, BLOCKS - 1) as i:
            stage(i + 1)
            first(i + 1)
            second(i)
        second(BLOCKS - 1)

    @block.vector
    def _(dve):
        count = dve.alloc_register("route_count")
        dve.wait_ge(w_hi, 1)
        nc.vector.tensor_tensor(w_r1_lo[:], w_r1, w_r1_hi[:].bitcast(F32), ALU.subtract).then_inc(w_lo, 1)

        def first(i):
            tiles = ds(i * BT, BT)
            dve.wait_ge(o_ready, i + 1)
            nc.vector.tensor_tensor(x_sb[:, tiles, :].rearrange("p t f -> p (t f)"),
                                    ps_w.rearrange("p b f -> p (b f)"),
                                    x_sb[:, tiles, :].rearrange("p t f -> p (t f)"), ALU.add).then_inc(residual, 1)
            wait_apart(dve, count, residual, i + 1, w_lo, 1)
            for t in range(BT):
                last = nc.vector.bn_stats(stats[:, t, :], x_sb[:, ds(i * BT + t, 1), :].squeeze(1))
            last.then_inc(stat_step, 1)
            wait_apart(dve, count, stat_step, 2 * i + 1, w_lo, 1)
            for t in range(BT):
                last = nc.vector.bn_aggr(mv[:, t, :], stats[:, t, :])
            last.then_inc(stat_step, 1)
            dve.wait_ge(stat_step, 2 * i + 2)
            nc.vector.tensor_scalar_add(var[:], mv[:, :, 1], LN_EPS).then_inc(var_ready, 1)
            dve.wait_ge(rstd_ready, i + 1)
            dve.wait_ge(t_ready, i)
            for t in range(BT):
                last = nc.vector.tensor_scalar(xn[:, t, :], x_sb[:, ds(i * BT + t, 1), :].squeeze(1),
                                               mv[:, t, 0:1], rstd[:, t:t + 1], ALU.subtract, ALU.mult)
            last.then_inc(xn_ready, 1)

        def second(i):
            cols = ds(i * BLOCK, BLOCK)
            dve.wait_ge(hi_ready, i + 1)
            nc.vector.tensor_tensor(xT_lo[:, :, cols], ps_t, xT_hi[:, :, cols].bitcast(F32), ALU.subtract
                                    ).then_inc(lo_ready, 1)
            dve.wait_ge(lg_tr, i + 1)
            nc.vector.tensor_reduce(logits[:, ds(i * BT, BT), :],
                                    ps_r[1].rearrange("p (c j e) -> p c e j", c=BT, j=MR)[:, :, 0:EXPERTS, :],
                                    axis=AXIS.X, op=ALU.add).then_inc(lg_read, 1)

        first(0)
        with dve.Fori(0, BLOCKS - 1) as i:
            first(i + 1)
            second(i)
        second(BLOCKS - 1)

    @block.tensor
    def _(pe):
        pe.wait_ge(const_in, 16 * CONSTS)
        pe.wait_ge(w_lo, 1)

        def first(i):
            pe.wait_ge(band_in, 16 * (i + 1))
            pe.wait_ge(staged, i + 1)
            for m in range(KD):
                pe.wait_ge(a_copied[m], i)
                feats = slice(m * P, (m + 1) * P)
                for t in range(BT):
                    nc.tensor.matmul(ps_a[m][:, t * P:(t + 1) * P], o_st[:, t, feats], jump[:],
                                     start=t == 0, stop=False)
                for t in range(BT):
                    q0, q1 = max(0, t * P - WINDOW), min(BLOCK, (t + 1) * P + WINDOW)
                    c0 = t * WIN + q0 - (t * P - WINDOW)
                    nc.tensor.matmul(ps_a[m][:, q0:q1], v_st[:, t, feats], band[:, c0:c0 + q1 - q0],
                                     start=False, stop=False)
                for q0, c0 in ((0, BT * WIN), (BLOCK - WINDOW, BT * WIN + WINDOW)):
                    last = nc.tensor.matmul(ps_a[m][:, q0:q0 + WINDOW], v_halo[:, feats], band[:, c0:c0 + WINDOW],
                                            start=False, stop=q0 > 0)
                last.then_inc(a_ready[m], 1)
            for m in range(KD):
                pe.wait_ge(a_copied[m], i + 1)
            pe.wait_ge(residual, i)
            for t in range(BT):
                for k in range(KD):
                    last = nc.tensor.matmul(ps_w[:, t // 2, (t % 2) * DIM:(t % 2 + 1) * DIM],
                                            attnT[:, k, t * P:(t + 1) * P], w_o[:, k, :],
                                            start=k == 0, stop=k == KD - 1)
            last.then_inc(o_ready, 1)

        def second(i):
            pe.wait_ge(xn_ready, i + 1)
            pe.wait_ge(lo_ready, i)
            for k in range(KD):
                for t in range(BT):
                    last = nc.tensor.transpose(ps_t[:, k, t * P:(t + 1) * P], xn[:, t, k * P:(k + 1) * P], ident[:])
            last.then_inc(t_ready, 1)
            pe.wait_ge(lo_ready, i + 1)
            cols = ds(i * BLOCK, BLOCK)
            for m in range(MR):
                if m == 0:
                    pe.wait_ge(lg_copied, i)
                elif m == 1:
                    pe.wait_ge(lg_read, i)
                else:
                    pe.wait_ge(rh_ready[m - 2], i + 1)
                feats = slice(m * P, (m + 1) * P)
                terms = [(w, xs, k) for w, xs in ((w_r1_hi, xT_hi), (w_r1_hi, xT_lo), (w_r1_lo, xT_hi))
                         for k in range(KD)]
                for n, (w, xs, k) in enumerate(terms):
                    last = nc.tensor.matmul(ps_r[m % 2], w[:, k, feats], xs[:, k, cols],
                                            start=n == 0, stop=n == len(terms) - 1)
                last.then_inc(r_ready[m], 1)
            for m in range(MR):
                pe.wait_ge(rh_ready[m], i + 1)
            for m in range(MR):
                last = nc.tensor.matmul(ps_r[0][m * QUAD:(m + 1) * QUAD, :], w_r2[:, m, :], rh[:, m, :],
                                        start=True, stop=True)
            last.then_inc(lg_ready, 1)
            pe.wait_ge(lg_copied, i + 1)
            for c in range(BT):
                last = nc.tensor.transpose(ps_r[1][:, c * P:(c + 1) * P], logitsT[:, c * P:(c + 1) * P], ident[:])
            last.then_inc(lg_tr, 1)

        steps(pe, first, second)


def experts(nc, ctx, dram, keep):
    def sb(name, shape, dt=F32):
        return ctx.enter_context(nc.sbuf_tensor(name, shape, dt))

    def sem(name):
        return ctx.enter_context(nc.semaphore(name))

    x_sb, xT_hi, xT_lo, logits = (keep[n] for n in ("x", "xT_hi", "xT_lo", "logits"))
    raw1 = sb("raw1", [P, KD, HIDDEN])
    raw2 = sb("raw2", [P, MH, DIM])
    w1 = [(sb(f"w1_hi{u}", [P, KD, HIDDEN], F32R), sb(f"w1_lo{u}", [P, KD, HIDDEN], F32R)) for u in range(2)]
    w2 = [(sb(f"w2_hi{u}", [P, MH, DIM], F32R), sb(f"w2_lo{u}", [P, MH, DIM], F32R)) for u in range(2)]
    b1 = sb("b1", [P, EXPERTS, MH])
    b2 = sb("b2", [P, EXPERTS, DIM])
    b_r2 = sb("b_r2", [P, EXPERTS])
    before = sb("before", [P, 2, EXPERTS, EXPERTS])
    h = [sb(f"h{c}", [P, BLOCK]) for c in range(2)]
    h_hi = [sb(f"h_hi{c}", [P, BLOCK], F32R) for c in range(4)]
    h_lo = [sb(f"h_lo{c}", [P, BLOCK], F32R) for c in range(4)]
    NT = [P, TILES]
    top = sb("top", NT)
    prob = sb("prob", [P, TILES, EXPERTS])
    cmp = [sb(f"cmp{c}", [P, TILES, EXPERTS, EXPERTS]) for c in range(1)]
    cmp.append(h[0][:].rearrange("p (t e j) -> p t e j", e=EXPERTS, j=EXPERTS))
    rank = sb("rank", [P, TILES, EXPERTS])
    gate = sb("gate", [P, TILES, EXPERTS])
    psum = ctx.enter_context(nc.psum_tensor("psum_experts", [P, 8, BLOCK], F32))
    ps_h = [psum[:, c, :] for c in range(2)]
    ps_y = [psum[:, 2 + t, 0:DIM] for t in range(BT)]

    const_in = sem("expert_const_in")
    raw_in, hi_set, lo_set = sem("raw_in"), sem("weights_hi"), sem("weights_lo")
    gate_step, shifted, exp_ready = sem("gate_step"), sem("shifted"), sem("exp_ready")
    h_ready = [sem(f"h_ready{c}") for c in range(2)]
    gelu_done = [sem(f"gelu_done{c}") for c in range(2)]
    h_hi_ready = sem("h_hi_ready")
    h_lo_ready = [sem(f"h_lo_ready{c}") for c in range(2)]
    h_used = [sem(f"h_used{c}") for c in range(4)]
    y_ready = [sem(f"y_ready{t}") for t in range(BT - 1)]
    y_read = [sem(f"y_read{t}") for t in range(BT)]
    acc_done, out_stored = sem("acc_done"), sem("out_stored")
    CONSTS = 4

    block = ctx.enter_context(nc.Block())

    @block.sync
    def _(sp):
        for e in range(EXPERTS):
            sp.wait_ge(lo_set, 2 * e)
            sp.dma_start(raw1[:], dram["We1"][e].rearrange("(k p) n -> p k n", p=P)).then_inc(raw_in, 16)
            sp.dma_start(raw2[:], dram["We2"][e].rearrange("(k p) n -> p k n", p=P)).then_inc(raw_in, 16)
            if e == 0:
                for dst, src in ((b1[:], dram["be1"]), (b2[:], dram["be2"].rearrange("(o e) f -> o e f", o=1)
                                                        .partition_broadcast(P)),
                                 (b_r2[:], dram["rb2"].rearrange("(o e) -> o e", o=1).partition_broadcast(P)),
                                 (before[:], dram["before"].rearrange("(o c) e j -> o c e j", o=1)
                                  .partition_broadcast(P))):
                    sp.dma_start(dst, src).then_inc(const_in, 16)
        with sp.Fori(0, BLOCKS) as i:
            sp.wait_ge(acc_done, (EXPERTS - 1) * BLOCKS + i + 1)
            sp.dma_start(dram["out"].rearrange("(n p) f -> p n f", p=P)[:, ds(i * BT, BT), :],
                         x_sb[:, ds(i * BT, BT), :]).then_inc(out_stored, 16)
        sp.wait_ge(out_stored, 16 * BLOCKS)

    @block.gpsimd
    def _(pool):
        for e in range(1, EXPERTS):
            pool.wait_ge(raw_in, 32 * (e + 1))
            if e >= 2:
                pool.wait_ge(h_used[3], 2 * BLOCKS * (e - 1))
            for n, (raw, w) in enumerate(((raw1, w1), (raw2, w2))):
                nc.gpsimd.tensor_copy(w[e % 2][0][:], raw[:]).then_inc(hi_set, 1)
                pool.wait_ge(hi_set, 2 * e + n + 1)
                nc.gpsimd.tensor_tensor(w[e % 2][1][:], raw[:], w[e % 2][0][:].bitcast(F32), ALU.subtract
                                        ).then_inc(lo_set, 1)
                pool.wait_ge(lo_set, 2 * e + n + 1)

    @block.scalar
    def _(act):
        act.wait_ge(shifted, 1)
        nc.scalar.activation(prob[:], prob[:], ACT.Exp).then_inc(exp_ready, 1)
        act.wait_ge(raw_in, 32)
        for n, (raw, w) in enumerate(((raw1, w1), (raw2, w2))):
            nc.scalar.activation(w[0][0][:], raw[:], ACT.Copy).then_inc(hi_set, 1)
        act.wait_ge(const_in, 16 * CONSTS)
        act.wait_ge(gate_step, GATE_STEPS)
        for e in range(EXPERTS):
            with act.Fori(0, BLOCKS) as b:
                n = e * BLOCKS + b
                for m in range(MH):
                    act.wait_ge(h_ready[m % 2], MH // 2 * n + m // 2 + 1)
                    act.wait_ge(h_lo_ready[m % 2], MH // 2 * n + m // 2)
                    nc.scalar.activation(h[m % 2][:], ps_h[m % 2], ACT.Gelu, bias=b1[:, e, m:m + 1]
                                         ).then_inc(gelu_done[m % 2], 1)

    @block.vector
    def _(dve):
        done = [0]

        def gate_op(instruction):
            instruction.then_inc(gate_step, 1)
            done[0] += 1
            dve.wait_ge(gate_step, done[0])

        per_tile = [P, TILES, EXPERTS]
        pairs = [P, TILES, EXPERTS, EXPERTS]
        dve.wait_ge(const_in, 16 * CONSTS)
        gate_op(nc.vector.tensor_tensor(logits[:], logits[:], b_r2[:].unsqueeze(1).broadcast_to(per_tile), ALU.add))
        gate_op(nc.vector.tensor_reduce(top[:], logits[:], axis=AXIS.X, op=ALU.max))
        nc.vector.tensor_tensor(prob[:], logits[:], top[:].unsqueeze(2).broadcast_to(per_tile), ALU.subtract
                                ).then_inc(shifted, 1)
        dve.wait_ge(exp_ready, 1)
        gate_op(nc.vector.tensor_reduce(top[:], prob[:], axis=AXIS.X, op=ALU.add))
        gate_op(nc.vector.reciprocal(top[:], top[:]))
        gate_op(nc.vector.tensor_tensor(prob[:], prob[:], top[:].unsqueeze(2).broadcast_to(per_tile), ALU.mult))
        p_j, p_e = prob[:].unsqueeze(2).broadcast_to(pairs), prob[:].unsqueeze(3).broadcast_to(pairs)
        for c, op in enumerate((ALU.is_gt, ALU.is_ge)):
            scratch = cmp[c] if c else cmp[c][:]
            gate_op(nc.vector.tensor_tensor(scratch, p_j, p_e, op))
            gate_op(nc.vector.tensor_tensor(scratch, scratch, before[:, c].unsqueeze(1).broadcast_to(pairs),
                                            ALU.mult))
        gate_op(nc.vector.tensor_tensor(cmp[1], cmp[1], cmp[0][:], ALU.add))
        gate_op(nc.vector.tensor_reduce(rank[:], cmp[1], axis=AXIS.X, op=ALU.add))
        gate_op(nc.vector.tensor_scalar(rank[:], rank[:], 1.5, None, ALU.is_lt))
        gate_op(nc.vector.tensor_tensor(gate[:], prob[:], rank[:], ALU.mult))
        assert done[0] == GATE_STEPS
        for n, (raw, w) in enumerate(((raw1, w1), (raw2, w2))):
            dve.wait_ge(hi_set, n + 1)
            nc.vector.tensor_tensor(w[0][1][:], raw[:], w[0][0][:].bitcast(F32), ALU.subtract).then_inc(lo_set, 1)

        def halves(n, m):
            s = MH * n + m
            dve.wait_ge(gelu_done[m % 2], MH // 2 * n + m // 2 + 1)
            dve.wait_ge(h_used[m % 4], MH // 4 * n + m // 4)
            nc.vector.tensor_copy(h_hi[m % 4][:], h[m % 2][:]).then_inc(h_hi_ready, 1)
            dve.wait_ge(h_hi_ready, s + 1)
            nc.vector.tensor_tensor(h_lo[m % 4][:], h[m % 2][:], h_hi[m % 4][:].bitcast(F32), ALU.subtract
                                    ).then_inc(h_lo_ready[m % 2], 1)

        def accumulate(e, b):
            n = e * BLOCKS + b
            dve.wait_ge(acc_done, n)
            for t in range(BT):
                acc, g = x_sb[:, ds(b * BT + t, 1), :].squeeze(1), gate[:, ds(b * BT + t, 1), e]
                if t < BT - 1:
                    dve.wait_ge(y_ready[t], n + 1)
                else:
                    dve.wait_ge(h_used[3], 2 * (n + 1))
                nc.vector.scalar_tensor_tensor(acc, ps_y[t], g, acc, ALU.mult, ALU.add).then_inc(y_read[t], 1)
            for t in range(BT):
                acc, g = x_sb[:, ds(b * BT + t, 1), :].squeeze(1), gate[:, ds(b * BT + t, 1), e]
                dve.wait_ge(y_read[t], n + 1)
                last = nc.vector.scalar_tensor_tensor(acc, b2[:, e, :], g, acc, ALU.mult, ALU.add)
            last.then_inc(acc_done, 1)

        halves(0, 0)
        for e in range(EXPERTS):
            def body(b, last):
                n = e * BLOCKS + b
                for m in range(1, MH):
                    halves(n, m)
                if not (last and e == EXPERTS - 1):
                    halves(n + 1, 0)
                accumulate(e, b)

            twice(dve, BLOCKS, body)

    @block.tensor
    def _(pe):
        def hidden(e, b, m):
            n = e * BLOCKS + b
            pe.wait_ge(gelu_done[m % 2], MH // 2 * n + m // 2)
            feats, cols = slice(m * P, (m + 1) * P), ds(b * BLOCK, BLOCK)
            hi, lo = w1[e % 2]
            terms = [(w, xs, k) for w, xs in ((hi, xT_hi), (hi, xT_lo), (lo, xT_hi)) for k in range(KD)]
            for j, (w, xs, k) in enumerate(terms):
                last = nc.tensor.matmul(ps_h[m % 2], w[:, k, feats], xs[:, k, cols],
                                        start=j == 0, stop=j == len(terms) - 1)
            last.then_inc(h_ready[m % 2], 1)

        def output(e, b, m):
            n = e * BLOCKS + b
            hi, lo = w2[e % 2]
            pe.wait_ge(h_lo_ready[m % 2], MH // 2 * n + m // 2 + 1)
            for t in range(BT):
                toks = slice(t * P, (t + 1) * P)
                if m == 0:
                    pe.wait_ge(y_read[t], n)
                terms = ((h_hi, hi), (h_hi, lo), (h_lo, hi))
                for j, (hs, w) in enumerate(terms):
                    last = nc.tensor.matmul(ps_y[t], hs[m % 4][:, toks], w[:, m, :],
                                            start=m == 0 and j == 0, stop=m == MH - 1 and j == 2)
                if t == BT - 1:
                    last.then_inc(h_used[m % 4], 1)
                elif m == MH - 1:
                    last.then_inc(y_ready[t], 1)

        pe.wait_ge(lo_set, 1)
        hidden(0, 0, 0)
        pe.wait_ge(lo_set, 2)
        for e in range(EXPERTS):
            def body(b, last):
                for m in range(MH):
                    if m < MH - 1:
                        hidden(e, b, m + 1)
                    elif not last:
                        hidden(e, b + 1, 0)
                    elif e < EXPERTS - 1:
                        pe.wait_ge(lo_set, 2 * (e + 2))
                        hidden(e + 1, 0, 0)
                    output(e, b, m)

            twice(pe, BLOCKS, body)


def program(nc, dram):
    with ExitStack() as whole:
        def sb(name, shape, dt=F32):
            return whole.enter_context(nc.sbuf_tensor(name, shape, dt))

        keep = {
            "x": sb("x_sb", [P, TILES, DIM]), "ident": sb("ident_sb", [P, P]), "jump": sb("jump_sb", [P, P]),
            "ident16": sb("ident16", [P, P], BF16), "logits": sb("logits", [P, TILES, EXPERTS]),
        }
        dram["qk_pieces"] = nc.dram_tensor("qk_pieces", (2, NHEADS, PIECES, HD, SEQ), BF16, kind="Internal").ap()
        with ExitStack() as tokens:
            keep["v"] = tokens.enter_context(nc.sbuf_tensor("v_sb", [P, NHEADS, ST + 2, HD], F32))
            keep["o"] = tokens.enter_context(nc.sbuf_tensor("o_sb", [P, NHEADS + 1, ST, HD], F32))
            for stage in (project, attend):
                with ExitStack() as ctx:
                    stage(nc, ctx, dram, keep)
            for n in ("xT_hi", "xT_lo"):
                keep[n] = whole.enter_context(nc.sbuf_tensor(n, [P, KD, TOKENS], F32R, side="right"))
            with ExitStack() as ctx:
                route(nc, ctx, dram, keep)
        with ExitStack() as ctx:
            experts(nc, ctx, dram, keep)


def local_band():
    q, t = np.arange(SEQ)[:, None], np.arange(SEQ)[None, :]
    d = (q - t).astype(np.float32)
    k = np.where(np.abs(d) <= WINDOW, np.exp(-d ** 2 / np.float32(2.0 * LOCAL_STRENGTH ** 2)), np.float32(0))
    k = (np.float32(1.0 - JUMP) * (k / (k.sum(-1, keepdims=True, dtype=np.float32) + np.float32(EPS)))).astype(np.float32)
    padded = np.zeros((SEQ + 2 * P, SEQ + 2 * P), np.float32)
    padded[P:-P, P:-P] = k
    band = np.zeros((BPS, P, BAND), np.float32)
    for j in range(BPS):
        start = P + j * BLOCK
        for t in range(BT):
            key = start + t * P
            band[j, :, t * WIN:(t + 1) * WIN] = padded[key - WINDOW:key + P + WINDOW, key:key + P].T
        halo = band[j, :, BT * WIN:]
        halo[96:, 0:WINDOW] = padded[start:start + WINDOW, start - P:start].T[96:]
        end = start + BLOCK
        halo[:96, WINDOW:] = padded[end - WINDOW:end, end:end + P].T[:96]
    return band


def kernel(**inputs):
    import concourse.bacc as bacc
    from concourse.bass_utils import run_bass_kernel_spmd

    a = {n.split("_", 2)[2]: np.asarray(v) for n, v in inputs.items() if n.startswith("L0_attn_")}
    f = {n.split("_", 2)[2]: np.asarray(v) for n, v in inputs.items() if n.startswith("L0_ffn_")}
    eye = np.eye(P, dtype=np.float32)
    j, e = np.arange(EXPERTS)[None, :], np.arange(EXPERTS)[:, None]
    w_r2 = np.zeros((RHID, QUAD), np.float32)
    w_r2[:, :EXPERTS] = f["rW2"]

    def columns(v):
        return v.reshape(-1, P).T

    arrays = {
        "x": a["x"].reshape(TOKENS, DIM),
        "wqT": a["Wq"].T, "wkT": a["Wk"].T, "wvT": a["Wv"].T, "woT": a["Wo"].T,
        "bq": columns(a["bq"]), "bk": columns(a["bk"]), "bv": a["bv"], "bo": a["bo"],
        "rW1": f["rW1"], "rb1": columns(f["rb1"]), "rW2": w_r2, "rb2": f["rb2"],
        "We1": f["We1"], "be1": f["be1"].reshape(EXPERTS, MH, P).transpose(2, 0, 1), "We2": f["We2"], "be2": f["be2"],
        "ident": eye, "jump": np.float32(JUMP) * eye, "band": local_band(),
        "before": np.stack([j > e, j < e]).astype(np.float32),
    }
    nc = bacc.Bacc("TRN2", target_bir_lowering=False, num_devices=1)
    arrays = {n: np.ascontiguousarray(v) for n, v in arrays.items()}
    dram = {n: nc.dram_tensor(f"in_{n}", v.shape, mybir.dt.from_np(v.dtype), kind="ExternalInput").ap()
            for n, v in arrays.items()}
    dram["out"] = nc.dram_tensor("out", (TOKENS, DIM), F32, kind="ExternalOutput").ap()
    program(nc, dram)
    r = run_bass_kernel_spmd(nc, [{f"in_{n}": v for n, v in arrays.items()}], core_ids=[0])
    return r.results[0]["out"].reshape(BATCH, SEQ, DIM)
```

```python
from contextlib import ExitStack

import numpy as np

import concourse.bass as bass
from concourse import mybir

F32 = mybir.dt.float32
F32R = mybir.dt.float32r
BF16 = mybir.dt.bfloat16
ALU = mybir.AluOpType
ACT = mybir.ActivationFunctionType
AXIS = mybir.AxisListType

P = 128
BATCH, SEQ, DIM = 2, 2048, 256
HEADS = 16
HD = DIM // HEADS
TOKENS = BATCH * SEQ
TILES = TOKENS // P
BT = 4
BLOCK = BT * P
BLOCKS = TOKENS // BLOCK
BPS = SEQ // BLOCK
ST = SEQ // P
KD = DIM // P
NHEADS = BATCH * HEADS
EXPERTS, HIDDEN, RHID = 4, 1024, 512
MH = HIDDEN // P
MR = RHID // P
JUMP, LOCAL_STRENGTH, WINDOW, EPS = 0.6, 0.4, 3, 1e-10
LN_EPS = 1e-5
PIECES = 3
PIECE_RUNS = (3, 2, 1)
STACK = HD * sum(PIECE_RUNS)
STACK_DMAS = 2 * len(PIECE_RUNS)
SROWS = STACK + PIECES
WIN = P + 2 * WINDOW
BAND = BT * WIN + 2 * WINDOW
LOOK = 20
SHIFT_AT = 13
QUAD = 32


def ds(start, size):
    return bass.ds(start, size)


def twice(engine, pairs, body):
    with engine.Fori(0, pairs - 1) as i:
        body(i, False)
    body(pairs - 1, True)


def wait_apart(engine, count, sem, value, held, held_value):
    if isinstance(value, int):
        engine.wait_ge(sem, value)
    else:
        engine.reg_mov(count, value)
        engine.wait_ge(held, held_value)
        engine.wait_ge(sem, count)


def load_stack(sp, dram, q_stack, k_stack, n, signal):
    row = 0
    for j, run in enumerate(PIECE_RUNS):
        span = slice(row, row + run * HD)
        sp.dma_start(q_stack[span, :], dram["qk_pieces"][0, ds(n, 1), :, 0:run, :].squeeze(0)
                     .rearrange("d c t -> c d t")).then_inc(signal, 16)
        sp.dma_start(k_stack[span, :], dram["qk_pieces"][1, ds(n, 1), :, j:j + 1, :].squeeze(0)
                     .rearrange("d c t -> c d t").broadcast_to([run, HD, SEQ])).then_inc(signal, 16)
        row += run * HD


def project(nc, ctx, dram, keep):
    def sb(name, shape, dt=F32):
        return ctx.enter_context(nc.sbuf_tensor(name, shape, dt))

    def sem(name):
        return ctx.enter_context(nc.semaphore(name))

    x_sb, v_sb, ident, max_q, max_k = (keep[n] for n in ("x", "v", "ident", "max_q0", "max_k0"))
    w = {"q": sb("w_q", [P, KD, DIM]), "k": sb("w_k", [P, KD, DIM]), "v": keep["w_v"]}
    bias_v, xnT = keep["bias_v"], keep["xnT"]
    bias_qk = sb("bias_qk", [P, 2, KD])
    half = sb("half", [P, BT])
    stats = [sb(f"stats{u}", [P, BT, 6]) for u in range(2)]
    mv = [sb(f"mv{u}", [P, BT, 2]) for u in range(2)]
    var = [sb(f"var{u}", [P, BT]) for u in range(2)]
    rstd = [sb(f"rstd{u}", [P, BT]) for u in range(2)]
    xn = [sb(f"xn{u}", [P, BT, DIM]) for u in range(2)]
    pieces = [sb(f"pieces{u}", [P, 2, KD, PIECES, BLOCK], BF16) for u in range(2)]
    rest = [sb(f"rest{j}", [P, BLOCK]) for j in range(2 * KD)]
    psum = ctx.enter_context(nc.psum_tensor("psum_project", [P, 8, BLOCK], F32))
    ps_t = psum[:, 0:2, :]
    ps_qk = [psum[:, 4 + j, :] for j in range(2 * KD)]
    QK = 2 * KD
    BETWEEN = 2

    ident_in, weights_in, biases_in, pool_set = sem("ident_in"), sem("weights_in"), sem("biases_in"), sem("pool_set")
    x_in = [sem(f"x_in{u}") for u in range(2)]
    stats_done, mv_done, var_ready, rstd_ready = sem("stats_done"), sem("mv_done"), sem("var_ready"), sem("rstd_ready")
    xn_ready, t_ready, xnT_ready = sem("xn_ready"), sem("t_ready"), sem("xnT_ready")
    qk_ready, piece1, qk_read, piece2, piece3 = (sem(n) for n in (
        "qk_ready", "piece1", "qk_read", "piece2", "piece3"))
    stored = [sem(f"stored{u}") for u in range(2)]
    first_stack = sem("first_stack")
    pairs = BLOCKS // 2

    def peeled(engine, body):
        body(0, True, False)
        with engine.Fori(1, pairs - 1) as i:
            body(i, False, False)
        body(pairs - 1, False, True)

    block = ctx.enter_context(nc.Block())

    @block.sync
    def _(sp):
        def load_x(n, u):
            sp.dma_start(x_sb[:, ds(n * BT, BT), :],
                         dram["x"].rearrange("(n p) f -> p n f", p=P)[:, ds(n * BT, BT), :]).then_inc(x_in[u], 16)

        def load_w(n, signal):
            sp.dma_start(w[n][:], dram[f"w{n}T"].rearrange("(k p) n -> p k n", p=P)).then_inc(signal, 16)

        load_x(0, 0)
        sp.dma_start(ident[:], dram["ident"]).then_inc(ident_in, 16)
        load_w("q", weights_in)
        load_x(1, 1)
        load_w("k", weights_in)
        for dst, src in ((bias_qk[:, 0, :], dram["bq"]), (bias_qk[:, 1, :], dram["bk"]),
                         (bias_v[:], dram["bv"].rearrange("(o f) -> o f", o=1).partition_broadcast(P)),
                         (keep["jump"][:], dram["jump"])):
            sp.dma_start(dst, src).then_inc(biases_in, 16)
        load_w("v", biases_in)
        with sp.Fori(1, pairs) as i:
            for u in range(2):
                sp.wait_ge(x_in[u], 16 * i)
                load_x(2 * i + u, u)
        for seq in range(BATCH):
            with sp.Fori(seq * BPS // 2, (seq + 1) * BPS // 2) as i:
                for u in range(2):
                    n = 2 * i + u
                    for qk in range(2):
                        for m in range(KD):
                            sp.wait_ge(piece3, QK * n + 2 * qk + m + 1)
                            head = seq * HEADS + m * (HEADS // KD)
                            dst = dram["qk_pieces"][qk, head:head + HEADS // KD, :, :, ds((n % BPS) * BLOCK, BLOCK)]
                            sp.dma_start(dst.rearrange("h d c t -> (h d) c t"), pieces[u][:, qk, m, :, :]
                                         ).then_inc(stored[u], 16)
            for u in range(2):
                sp.wait_ge(stored[u], 16 * QK * (seq + 1) * BPS // 2)
            if seq == 0:
                load_stack(sp, dram, max_q, max_k, 0, first_stack)
        sp.wait_ge(first_stack, 16 * STACK_DMAS)

    @block.gpsimd
    def _(pool):
        nc.gpsimd.memset(half[:], -0.5).then_inc(pool_set, 1)
        nc.gpsimd.memset(v_sb[:, :, 0, :], 0.0).then_inc(pool_set, 1)
        nc.gpsimd.memset(v_sb[:, :, ST + 1, :], 0.0).then_inc(pool_set, 1)
        pool.wait_ge(pool_set, 3)
        with pool.Fori(0, pairs) as i:
            for u in range(2):
                pool.wait_ge(var_ready, 2 * i + u + 1)
                nc.gpsimd.tensor_tensor(rstd[u][:], var[u][:], half[:], ALU.pow).then_inc(rstd_ready, 1)

    @block.vector
    def _(dve):
        count = dve.alloc_register("project_count")

        def statistics(i, u):
            n = 2 * i + u
            wait_apart(dve, count, x_in[u], 16 * (i + 1), pool_set, 1)
            for t in range(BT):
                last = nc.vector.bn_stats(stats[u][:, t, :], x_sb[:, ds(n * BT + t, 1), :].squeeze(1))
            last.then_inc(stats_done, 1)
            wait_apart(dve, count, stats_done, n + 1, pool_set, 1)
            for t in range(BT):
                last = nc.vector.bn_aggr(mv[u][:, t, :], stats[u][:, t, :])
            last.then_inc(mv_done, 1)
            dve.wait_ge(mv_done, n + 1)
            nc.vector.tensor_scalar_add(var[u][:], mv[u][:, :, 1], LN_EPS).then_inc(var_ready, 1)

        def normalise(i, u):
            n = 2 * i + u
            dve.wait_ge(rstd_ready, n + 1)
            if not (isinstance(n, int) and n < 2):
                dve.wait_ge(t_ready, n - 1)
            for t in range(BT):
                last = nc.vector.tensor_scalar(xn[u][:, t, :], x_sb[:, ds(n * BT + t, 1), :].squeeze(1),
                                               mv[u][:, t, 0:1], rstd[u][:, t:t + 1], ALU.subtract, ALU.mult)
            last.then_inc(xn_ready, 1)

        def split_qk(n, u, meanwhile):
            for step in range(QK + BETWEEN):
                if step == 1:
                    meanwhile()
                j = step
                if j < QK:
                    if not (isinstance(n, int) and n == 0):
                        dve.wait_ge(piece3, QK * (n - 1) + j + 1)
                    dve.wait_ge(piece1, QK * n + j + 1)
                    nc.vector.scalar_tensor_tensor(rest[j][:], ps_qk[j], bias_qk[:, j // KD, j % KD:j % KD + 1],
                                                   pieces[u][:, j // KD, j % KD, 0, :], ALU.add, ALU.subtract
                                                   ).then_inc(qk_read, 1)
                j = step - BETWEEN
                if j >= 0:
                    piece = pieces[u][:, j // KD, j % KD, :, :]
                    dve.wait_ge(piece2, QK * n + j + 1)
                    nc.vector.tensor_tensor(piece[:, 2, :], rest[j][:], piece[:, 1, :], ALU.subtract
                                            ).then_inc(piece3, 1)

        dve.wait_ge(pool_set, 1)
        for u in range(2):
            statistics(0, u)
            normalise(0, u)
        dve.wait_ge(biases_in, 16 * 5)

        def body(i, first, last):
            for u in range(2):
                if last:
                    split_qk(2 * i + u, u, lambda: None)
                else:
                    statistics(i + 1, u)
                    split_qk(2 * i + u, u, lambda: normalise(i + 1, u))

        peeled(dve, body)

    @block.scalar
    def _(act):
        def copy_T(n):
            act.wait_ge(t_ready, n + 1)
            nc.scalar.activation(xnT[:, ds(n, 1), :, :].squeeze(1), ps_t, ACT.Copy).then_inc(xnT_ready, 1)

        copy_T(0)
        act.wait_ge(biases_in, 16 * 5)

        def body(i, first, last):
            for u in range(2):
                n = 2 * i + u
                if not first:
                    act.wait_ge(stored[u], 16 * QK * i)
                for step in range(QK + BETWEEN):
                    j = step
                    if j == KD and not (last and u):
                        copy_T(n + 1)
                    if j < QK:
                        act.wait_ge(qk_ready, QK * n + j + 1)
                        nc.scalar.activation(pieces[u][:, j // KD, j % KD, 0, :], ps_qk[j], ACT.Identity,
                                             bias=bias_qk[:, j // KD, j % KD:j % KD + 1]).then_inc(piece1, 1)
                    j = step - BETWEEN
                    if j >= 0:
                        act.wait_ge(qk_read, QK * n + j + 1)
                        nc.scalar.activation(pieces[u][:, j // KD, j % KD, 1, :], rest[j][:], ACT.Copy
                                             ).then_inc(piece2, 1)

        peeled(act, body)

    @block.tensor
    def _(pe):
        def transposes(n, u):
            pe.wait_ge(xn_ready, n + 1)
            if not (isinstance(n, int) and n == 0):
                pe.wait_ge(xnT_ready, n)
            for k in range(KD):
                for t in range(BT):
                    last = nc.tensor.transpose(ps_t[:, k, t * P:(t + 1) * P],
                                               xn[u][:, t, k * P:(k + 1) * P], ident[:])
            last.then_inc(t_ready, 1)

        pe.wait_ge(ident_in, 16)
        transposes(0, 0)
        pe.wait_ge(weights_in, 16 * 2)

        def body(i, first, last):
            for u in range(2):
                n = 2 * i + u
                pe.wait_ge(xnT_ready, n + 1)
                for qk in range(2):
                    if qk == 1 and not (last and u):
                        transposes(n + 1, 1 - u)
                    for m in range(KD):
                        j = 2 * qk + m
                        if not (first and u == 0):
                            pe.wait_ge(qk_read, QK * (n - 1) + j + 1)
                        for k in range(KD):
                            done = nc.tensor.matmul(ps_qk[j], w["qk"[qk]][:, k, m * P:(m + 1) * P],
                                                    xnT[:, ds(n, 1), k, :].squeeze(1),
                                                    start=k == 0, stop=k == KD - 1)
                        done.then_inc(qk_ready, 1)

        peeled(pe, body)


def attend(nc, ctx, dram, keep):
    def sb(name, shape, dt=F32):
        return ctx.enter_context(nc.sbuf_tensor(name, shape, dt))

    def sem(name):
        return ctx.enter_context(nc.semaphore(name))

    x_sb, v_sb, o_sb, ident, ident16 = (keep[n] for n in ("x", "v", "o", "ident", "ident16"))
    max_q = [keep["max_q0"], sb("max_q1", [STACK, SEQ], BF16)]
    max_k = [keep["max_k0"], sb("max_k1", [STACK, SEQ], BF16)]
    score_q = [sb(f"score_q{u}", [SROWS, SEQ], BF16) for u in range(2)]
    score_k = [sb(f"score_k{u}", [SROWS, SEQ], BF16) for u in range(2)]
    w_o, w_r1_hi, w_r1_lo, w_r2, b_r1 = (keep[n] for n in ("w_o", "w_r1_hi", "w_r1_lo", "w_r2", "b_r1"))
    w_v, bias_v, xnT = keep["w_v"], keep["bias_v"], keep["xnT"]
    w_r1 = sb("w_r1", [P, KD, RHID])
    bias_o = sb("bias_o", [P, DIM])
    v_ones = [sb(f"v_ones{u}", [P, ST, QUAD]) for u in range(2)]
    probs = [sb(f"probs{c}", [P, SEQ]) for c in range(2)]
    heads_sb = sb("heads_sb", [P, BLOCK])
    heads_tok = sb("heads_tok", [P, BLOCK])
    part_max = sb("part_max", [P, ST, 2])
    neg_max = sb("neg_max", [P, ST])
    shift = sb("shift", [P, PIECES, ST], BF16)
    shift_rest = sb("shift_rest", [P, ST])
    shift_row = sb("shift_row", [PIECES * ST, P], BF16)
    inv_sum = sb("inv_sum", [P, ST])
    psum = ctx.enter_context(nc.psum_tensor("psum_attend", [P, 8, BLOCK], F32))
    ps_s = [psum[:, c, :] for c in range(3)]
    ps_o = psum[:, 3, :]
    ps_m = [psum[:, 4:6, :], psum[:, 6:8, :]]
    ps_tr = psum[:, 7, :]
    ps_shift = ps_tr[0:PIECES * ST, 0:P // 2].bitcast(BF16)
    CH = BPS

    ones_set = sem("ones_set")
    v_ready, v_copied, v_biased = sem("v_ready"), sem("v_copied"), sem("v_biased")
    route_in, route_split = sem("route_in"), sem("route_split")
    max_in = [sem(f"max_in{u}") for u in range(2)]
    score_in = [sem(f"score_in{u}") for u in range(2)]
    shift_in = [sem(f"shift_in{u}") for u in range(2)]
    v_in = sem("v_in")
    m_ready, m_read = sem("m_ready"), sem("m_read")
    shift_step, shift_ready = sem("shift_step"), sem("shift_ready")
    shift_tr, shift_copied = sem("shift_tr"), sem("shift_copied")
    s_ready, exp_done = sem("s_ready"), sem("exp_done")
    pv_done = sem("pv_done")
    o_copied = sem("o_copied")
    o_tr, tok_copied = sem("o_tr"), sem("tok_copied")
    inv_ready = sem("inv_ready")
    tok_used = sem("tok_used")
    pairs = NHEADS // 2
    PV_OPEN = 2
    POOL_SET = 6
    VB = 2
    BANKS = VB * BLOCKS
    SHIFT_HALF = 2 * (ST + 1) + 1

    def v_tiles_before(half):
        return half * TILES // (2 * LOOK)

    BANKS_BEFORE_SHIFT = v_tiles_before(SHIFT_HALF) // 2

    def v_tiles(b, vb):
        return v_sb[:, ds((b // BPS) * HEADS, HEADS), ds(1 + (b % BPS) * BT + 2 * vb, 2), :].rearrange(
            "p h t d -> p t h d")

    block = ctx.enter_context(nc.Block())

    @block.sync
    def _(sp):
        def load_shift(m, u):
            sp.wait_ge(shift_copied, m + 1)
            for c in range(PIECES):
                sp.dma_start(score_q[u][STACK + c:STACK + c + 1, :].rearrange("o (t q) -> o t q", q=P),
                             shift_row[c * ST:(c + 1) * ST, :]).then_inc(shift_in[u], 16)

        load_stack(sp, dram, score_q[0], score_k[0], 0, score_in[0])
        load_stack(sp, dram, max_q[1], max_k[1], 1, max_in[1])
        load_stack(sp, dram, score_q[1], score_k[1], 1, score_in[1])
        for dst, src in ((w_o[:], dram["woT"].rearrange("(k p) n -> p k n", p=P)),
                         (w_r1[:], dram["rW1"].rearrange("(k p) n -> p k n", p=P)),
                         (w_r2[:], dram["rW2"].rearrange("(k p) n -> p k n", p=P)),
                         (b_r1[:], dram["rb1"]),
                         (bias_o[:], dram["bo"].rearrange("(o f) -> o f", o=1).partition_broadcast(P))):
            sp.dma_start(dst, src).then_inc(route_in, 16)
        load_shift(0, 0)

        def body(i, last):
            for u in range(2):
                n = 2 * i + u
                if not last:
                    sp.wait_ge(m_ready, 2 * ST * (n + 1))
                    load_stack(sp, dram, max_q[u], max_k[u], n + 2, max_in[u])
                if not (last and u):
                    load_shift(n + 1, 1 - u)
                if not last:
                    sp.wait_ge(s_ready, CH * ST * (n + 1))
                    load_stack(sp, dram, score_q[u], score_k[u], n + 2, score_in[u])

        twice(sp, pairs, body)

    @block.gpsimd
    def _(pool):
        for u in range(2):
            nc.gpsimd.memset(v_ones[u][:], 1.0).then_inc(ones_set, 1)
            pool.wait_ge(ones_set, 2 * u + 1)
            nc.gpsimd.memset(score_k[u][STACK:SROWS, :], 1.0).then_inc(ones_set, 1)
            pool.wait_ge(ones_set, 2 * u + 2)
        nc.gpsimd.tensor_copy(ident16[:], ident[:]).then_inc(ones_set, 1)
        pool.wait_ge(ones_set, 5)
        nc.gpsimd.memset(heads_sb[:], 1.0).then_inc(o_copied, 1)
        pool.wait_ge(o_copied, 1)

        def stage(n, u):
            nc.gpsimd.tensor_copy(v_ones[u][:, :, 0:HD], v_sb[:, ds(n, 1), 1:ST + 1, :].squeeze(1)
                                  ).then_inc(v_in, 1)

        def add_bias(b):
            for vb in range(VB):
                pool.wait_ge(v_copied, VB * b + vb + 1)
                nc.gpsimd.tensor_tensor(v_tiles(b, vb), v_tiles(b, vb),
                                        bias_v[:].rearrange("p (o h d) -> p o h d", o=1, d=HD)
                                        .broadcast_to([P, 2, HEADS, HD]), ALU.add).then_inc(v_biased, 1)

        with pool.Fori(0, BPS) as b:
            add_bias(b)
        pool.wait_ge(v_biased, VB * BPS)
        stage(0, 0)
        pool.wait_ge(v_in, 1)
        stage(1, 1)
        with pool.Fori(BPS, BLOCKS) as b:
            add_bias(b)
        pool.wait_ge(v_biased, VB * BLOCKS)
        pool.wait_ge(route_in, 16 * 5)
        nc.gpsimd.tensor_copy(w_r1_hi[:], w_r1[:]).then_inc(route_split, 1)
        pool.wait_ge(route_split, 1)
        nc.gpsimd.tensor_tensor(w_r1_lo[:], w_r1[:], w_r1_hi[:].bitcast(F32), ALU.subtract).then_inc(route_split, 1)
        pool.wait_ge(route_split, 2)
        nc.gpsimd.tensor_tensor(x_sb[:], x_sb[:], bias_o[:].unsqueeze(1).broadcast_to([P, TILES, DIM]),
                                ALU.add).then_inc(route_split, 1)
        pool.wait_ge(route_split, 3)
        with pool.Fori(0, pairs - 1) as i:
            for u in range(2):
                n = 2 * i + u
                pool.wait_ge(pv_done, ST * (n + 1) + PV_OPEN)
                pool.wait_ge(v_in, n + 2)
                stage(n + 2, u)

    @block.vector
    def _(dve):
        def maxima(g, t):
            for p in range(2):
                dve.wait_ge(m_ready, 2 * g + p + 1)
                nc.vector.tensor_reduce(part_max[:, t, p:p + 1], ps_m[p].rearrange("q b f -> q (b f)"),
                                        axis=AXIS.X, op=ALU.max).then_inc(m_read, 1)

        def split_shift(m):
            dve.wait_ge(m_read, 2 * ST * (m + 1))
            base = 5 * m
            nc.vector.tensor_reduce(neg_max[:], part_max[:], axis=AXIS.X, op=ALU.max, negate=True
                                    ).then_inc(shift_step, 1)
            dve.wait_ge(shift_step, base + 1)
            if not isinstance(m, int) or m > 0:
                dve.wait_ge(shift_tr, m)
            nc.vector.tensor_copy(shift[:, 0, :], neg_max[:]).then_inc(shift_step, 1)
            dve.wait_ge(shift_step, base + 2)
            nc.vector.tensor_tensor(shift_rest[:], neg_max[:], shift[:, 0, :], ALU.subtract).then_inc(shift_step, 1)
            dve.wait_ge(shift_step, base + 3)
            nc.vector.tensor_copy(shift[:, 1, :], shift_rest[:]).then_inc(shift_step, 1)
            dve.wait_ge(shift_step, base + 4)
            nc.vector.tensor_tensor(neg_max[:], shift_rest[:], shift[:, 1, :], ALU.subtract).then_inc(shift_step, 1)
            dve.wait_ge(shift_step, base + 5)
            nc.vector.tensor_copy(shift[:, 2, :], neg_max[:]).then_inc(shift_ready, 1)

        def normalise(n):
            tok = heads_tok[:].rearrange("p (c b e) -> p c b e", c=BT, b=BPS)
            inv = inv_sum[:].rearrange("p (c b) -> p c b", c=BT)
            dve.wait_ge(tok_copied, n + 1)
            nc.vector.reciprocal(inv, tok[:, :, :, HD]).then_inc(inv_ready, 1)
            dve.wait_ge(inv_ready, n + 1)
            out = o_sb[:, ds(n, 1), :, :].squeeze(1).rearrange("p (b c) d -> p c b d", c=BT)
            nc.vector.tensor_tensor(out, tok[:, :, :, 0:HD], inv.unsqueeze(3).broadcast_to([P, BT, BPS, HD]),
                                    ALU.mult).then_inc(tok_used, 1)

        for t in range(ST):
            maxima(t, t)
        split_shift(0)
        for t in range(LOOK - ST):
            maxima(ST + t, t)

        def body(i, last):
            for u in range(2):
                n = 2 * i + u
                for kb in range(ST):
                    ahead = kb + LOOK - ST
                    if not (last and u + ahead // ST > 0):
                        maxima(ST * (n + 1) + ahead, ahead % ST)
                    if kb == 1:
                        normalise(n)
                    if ahead == ST - 1 and not (last and u):
                        split_shift(n + 1)

        twice(dve, pairs, body)
        normalise(NHEADS)

    @block.scalar
    def _(act):
        act.sem_inc(pv_done, PV_OPEN)
        act.sem_inc(tok_used, 1)

        def exp(n, kb, c):
            j = CH * kb + c
            if c == 0:
                act.wait_ge(pv_done, ST * n + kb - 1 + PV_OPEN)
            act.wait_ge(s_ready, CH * ST * n + j + 1)
            nc.scalar.activation(probs[kb % 2][:, c * BLOCK:(c + 1) * BLOCK], ps_s[j % 3], ACT.Exp,
                                 scale=float(HD) ** -0.5).then_inc(exp_done, 1)

        def copy_shift(m):
            act.wait_ge(shift_tr, m + 1)
            nc.scalar.activation(shift_row[:], ps_shift, ACT.Copy).then_inc(shift_copied, 1)

        def copy_tok(n):
            act.wait_ge(tok_used, n + 1)
            act.wait_ge(o_tr, n + 1)
            nc.scalar.activation(heads_tok[:], ps_tr, ACT.Copy).then_inc(tok_copied, 1)

        def copy_v(b, vb):
            act.wait_ge(v_ready, VB * b + vb + 1)
            nc.scalar.activation(v_tiles(b, vb), ps_s[vb].rearrange("p (t h d) -> p t h d", t=2, d=HD), ACT.Copy
                                 ).then_inc(v_copied, 1)

        with act.Fori(0, BANKS_BEFORE_SHIFT // VB) as b:
            for vb in range(VB):
                copy_v(b, vb)
        for r in range(BANKS_BEFORE_SHIFT // VB * VB, BANKS):
            if r == BANKS_BEFORE_SHIFT:
                copy_shift(0)
            copy_v(r // VB, r % VB)
        for c in range(CH):
            exp(0, 0, c)

        def body(i, last):
            for u in range(2):
                n = 2 * i + u
                for kb in range(1, ST):
                    for c in range(CH):
                        if c == CH - 1 and kb == 1:
                            copy_tok(n)
                        if c == CH - 1 and kb == SHIFT_AT + 1 and not (last and u):
                            act.wait_ge(shift_in[u], 16 * PIECES * (i + 1))
                            copy_shift(n + 1)
                        exp(n, kb, c)
                if not (last and u):
                    for c in range(CH):
                        exp(n + 1, 0, c)
                act.wait_ge(o_tr, n + 1)
                act.wait_ge(pv_done, ST * (n + 1) + PV_OPEN)
                nc.scalar.activation(heads_sb[:], ps_o, ACT.Copy).then_inc(o_copied, 1)

        twice(act, pairs, body)
        copy_tok(NHEADS)

    @block.tensor
    def _(pe):
        count = pe.alloc_register("attend_count")

        def maxima(g, t, u, p):
            if not isinstance(g, int) or g > 0:
                pe.wait_ge(m_read, 2 * g + p - 1)
            for j in range(2):
                c = 2 * p + j
                last = nc.tensor.matmul(ps_m[p][:, j, :], max_q[u][:, t * P:(t + 1) * P],
                                        max_k[u][:, c * BLOCK:(c + 1) * BLOCK], start=True, stop=True)
            last.then_inc(m_ready, 1)

        def scores(n, kb, u, c):
            j = CH * kb + c
            g = CH * ST * n + j
            used = g if j == 0 else g - 2
            if not isinstance(used, int) or used > 0:
                pe.wait_ge(exp_done, used)
            nc.tensor.matmul(ps_s[j % 3], score_k[u][:, kb * P:(kb + 1) * P],
                             score_q[u][:, c * BLOCK:(c + 1) * BLOCK], start=True, stop=True).then_inc(s_ready, 1)

        def values(n, kb, u):
            pe.wait_ge(exp_done, CH * (ST * n + kb + 1))
            if kb == 0:
                pe.wait_ge(o_copied, n + 1)
            for j in range(BPS):
                last = nc.tensor.matmul(ps_o[QUAD * j:QUAD * (j + 1), :], v_ones[u][:, kb, :],
                                        probs[kb % 2][:, j * BLOCK:(j + 1) * BLOCK],
                                        start=kb == 0, stop=kb == ST - 1)
            last.then_inc(pv_done, 1)

        def transpose_shift(m):
            wait_apart(pe, count, shift_ready, m + 1, ones_set, POOL_SET - 1)
            nc.tensor.transpose(ps_shift, shift[:].rearrange("p c t -> p (c t)"), ident16[:]).then_inc(shift_tr, 1)

        def transpose_heads(n):
            pe.wait_ge(o_copied, n + 1)
            for c in range(BT):
                last = nc.tensor.transpose(ps_tr[:, c * P:(c + 1) * P], heads_sb[:, c * P:(c + 1) * P], ident[:])
            last.then_inc(o_tr, 1)

        def project_v(r, t):
            b, vb = r // VB, r % VB
            if t == 0 and r >= VB:
                pe.wait_ge(v_copied, r - VB + 1)
            toks = slice((2 * vb + t) * P, (2 * vb + t + 1) * P)
            for k in range(KD):
                last = nc.tensor.matmul(ps_s[vb][:, t * DIM:(t + 1) * DIM], xnT[:, b, k, toks], w_v[:, k, :],
                                        start=k == 0, stop=k == KD - 1)
            if t == 1:
                last.then_inc(v_ready, 1)

        for t in range(LOOK):
            if t == ST:
                pe.wait_ge(ones_set, POOL_SET - 1)
                pe.wait_ge(max_in[1], 16 * STACK_DMAS)
            for p in range(2):
                half = 2 * t + p
                if half == SHIFT_HALF:
                    pe.wait_ge(m_read, 2 * (ST + 1))
                    transpose_shift(0)
                    pe.wait_ge(shift_copied, 1)
                maxima(t, t % ST, t // ST, p)
                for vt in range(v_tiles_before(half), v_tiles_before(half + 1)):
                    project_v(vt // 2, vt % 2)
        pe.wait_ge(v_copied, BANKS)
        pe.wait_ge(score_in[0], 16 * STACK_DMAS)
        pe.wait_ge(shift_in[0], 16 * PIECES)
        for c in range(CH):
            scores(0, 0, 0, c)

        def body(i, last):
            for u in range(2):
                n = 2 * i + u
                pe.wait_ge(v_in, n + 1)
                for kb in range(ST):
                    ahead = kb + LOOK - ST
                    g, mu = ST * (n + 1) + ahead, (u + 1 + ahead // ST) % 2
                    more_maxima = not (last and u + ahead // ST > 0)
                    more_scores = not (last and u == 1 and kb == ST - 1)
                    nxt = (n, kb + 1, u) if kb < ST - 1 else (n + 1, 0, 1 - u)
                    if ahead == ST and more_maxima:
                        pe.wait_ge(max_in[mu], 16 * STACK_DMAS * (i + 1 + u))
                    if kb == ST - 1 and more_scores:
                        pe.wait_ge(score_in[1 - u], 16 * STACK_DMAS * (i + 1 + u))
                        pe.wait_ge(shift_in[1 - u], 16 * PIECES * (i + 1 + u))
                    if more_scores:
                        scores(*nxt, 0)
                    if more_maxima:
                        maxima(g, ahead % ST, mu, 0)
                    if more_scores:
                        for c in range(1, CH):
                            scores(*nxt, c)
                    transposes = kb == 0 or (kb == SHIFT_AT and not (last and u))
                    if transposes:
                        pe.wait_ge(m_read, 2 * g if more_maxima else 2 * ST * NHEADS)
                        if kb == 0:
                            transpose_heads(n)
                        else:
                            transpose_shift(n + 1)
                        values(n, kb, u)
                    if more_maxima:
                        if kb == 0:
                            pe.wait_ge(tok_copied, n + 1)
                        if kb == SHIFT_AT:
                            pe.wait_ge(shift_copied, n + 2)
                        maxima(g, ahead % ST, mu, 1)
                    if not transposes:
                        values(n, kb, u)

        twice(pe, pairs, body)
        pe.wait_ge(tok_copied, NHEADS)
        transpose_heads(NHEADS)


def route(nc, ctx, dram, keep):
    def sb(name, shape, dt=F32):
        return ctx.enter_context(nc.sbuf_tensor(name, shape, dt))

    def sem(name):
        return ctx.enter_context(nc.semaphore(name))

    x_sb, v_sb, o_sb, ident, jump = (keep[n] for n in ("x", "v", "o", "ident", "jump"))
    xT_hi, xT_lo, logits = keep["xT_hi"], keep["xT_lo"], keep["logits"]
    w_o, w_r1_hi, w_r1_lo, w_r2, b_r1 = (keep[n] for n in ("w_o", "w_r1_hi", "w_r1_lo", "w_r2", "b_r1"))
    band = sb("band", [P, BAND])
    half = sb("half_route", [P, BT])
    o_st = sb("o_st", [P, BT, DIM])
    v_st = sb("v_st", [P, BT, DIM])
    v_halo = sb("v_halo", [P, DIM])
    attnT = sb("attnT", [P, KD, BLOCK])
    stats = sb("stats_route", [P, BT, 6])
    mv = sb("mv_route", [P, BT, 2])
    var = sb("var_route", [P, BT])
    rstd = sb("rstd_route", [P, BT])
    xn = sb("xn_route", [P, BT, DIM])
    rh = sb("rh", [P, MR, BLOCK])
    logitsT = sb("logitsT", [P, BLOCK])
    psum = ctx.enter_context(nc.psum_tensor("psum_route", [P, 8, BLOCK], F32))
    ps_a = [psum[:, 0, :], psum[:, 1, :]]
    ps_w = psum[:, 2:4, :]
    ps_t = psum[:, 4:6, :]
    ps_r = [psum[:, 6, :], psum[:, 7, :]]

    half_set = sem("half_set")
    band_in, staged = sem("band_in"), sem("staged")
    a_ready = [sem(f"a_ready{m}") for m in range(KD)]
    a_copied = [sem(f"a_copied{m}") for m in range(KD)]
    o_ready, residual = sem("o_ready"), sem("residual")
    stat_step, var_ready, rstd_ready = sem("stat_step"), sem("route_var"), sem("route_rstd")
    xn_ready, t_ready, hi_ready, lo_ready = (sem(n) for n in ("route_xn", "route_t", "hi_ready", "lo_ready"))
    r_ready = [sem(f"r_ready{m}") for m in range(MR)]
    rh_ready = [sem(f"rh_ready{m}") for m in range(MR)]
    lg_ready, lg_copied, lg_tr, lg_read = (sem(n) for n in ("lg_ready", "lg_copied", "lg_tr", "lg_read"))

    block = ctx.enter_context(nc.Block())

    def steps(engine, step, ahead):
        step(0)
        with engine.Fori(1, BLOCKS - ahead) as i:
            step(i)
        for i in range(BLOCKS - ahead, BLOCKS):
            step(i)

    def at_end(i, ahead):
        return isinstance(i, int) and i + ahead >= BLOCKS

    def at_start(i):
        return isinstance(i, int) and i == 0

    @block.sync
    def _(sp):
        sp.dma_start(band[:], dram["band"][0]).then_inc(band_in, 16)
        with sp.Fori(1, BLOCKS) as i:
            sp.wait_ge(a_ready[KD - 1], i)
            sp.dma_start(band[:], dram["band"][ds(i % BPS, 1)].squeeze(0)).then_inc(band_in, 16)

    @block.gpsimd
    def _(pool):
        nc.gpsimd.memset(half[:], -0.5).then_inc(half_set, 1)
        pool.wait_ge(half_set, 1)
        with pool.Fori(0, BLOCKS) as i:
            pool.wait_ge(var_ready, i + 1)
            nc.gpsimd.tensor_tensor(rstd[:], var[:], half[:], ALU.pow).then_inc(rstd_ready, 1)

    @block.scalar
    def _(act):
        def stage(i):
            heads, kt = (i // BPS) * HEADS, (i % BPS) * BT
            if not at_start(i):
                act.wait_ge(a_ready[KD - 1], i)
            def tiles(src, at, n):
                return src[:, ds(heads, HEADS), ds(at, n), :].rearrange("p h t d -> p t h d")
            def to(dst):
                return dst[:].rearrange("p t (h d) -> p t h d", d=HD)
            nc.scalar.activation(to(o_st), tiles(o_sb[:, 1:NHEADS + 1], kt, BT), ACT.Copy)
            nc.scalar.activation(to(v_st), tiles(v_sb, kt + 1, BT), ACT.Copy)
            for p0, p1, at in ((0, 64, kt + BT + 1), (64, 96, kt + BT + 1), (96, P, kt)):
                last = nc.scalar.activation(v_halo[p0:p1, :].rearrange("p (h d) -> p h d", d=HD),
                                            v_sb[p0:p1, ds(heads, HEADS), ds(at, 1), :].squeeze(2), ACT.Copy)
            last.then_inc(staged, 1)

        def copy_heads(i):
            for m in range(KD):
                act.wait_ge(a_ready[m], i + 1)
                if m == 0 and not at_start(i):
                    act.wait_ge(o_ready, i)
                nc.scalar.activation(attnT[:, m, :], ps_a[m], ACT.Copy).then_inc(a_copied[m], 1)

        def copy_hi(i):
            act.wait_ge(t_ready, i + 1)
            nc.scalar.activation(xT_hi[:, :, ds(i * BLOCK, BLOCK)], ps_t, ACT.Copy).then_inc(hi_ready, 1)

        def step(i):
            for m in range(MR):
                act.wait_ge(r_ready[m], i + 1)
                nc.scalar.activation(rh[:, m, :], ps_r[m % 2], ACT.Gelu, bias=b_r1[:, m:m + 1]
                                     ).then_inc(rh_ready[m], 1)
            if not at_end(i, 1):
                copy_hi(i + 1)
            act.wait_ge(lg_ready, i + 1)
            nc.scalar.activation(logitsT[:], ps_r[0], ACT.Copy).then_inc(lg_copied, 1)
            if not at_end(i, 3):
                stage(i + 3)
                copy_heads(i + 3)

        for i in range(3):
            stage(i)
            copy_heads(i)
            if i == 1:
                copy_hi(0)
        steps(act, step, 3)

    @block.vector
    def _(dve):
        count = dve.alloc_register("route_count")
        dve.wait_ge(half_set, 1)

        def read_logits(i):
            dve.wait_ge(lg_tr, i + 1)
            nc.vector.tensor_reduce(logits[:, ds(i * BT, BT), :],
                                    ps_r[1].rearrange("p (c j e) -> p c e j", c=BT, j=MR)[:, :, 0:EXPERTS, :],
                                    axis=AXIS.X, op=ALU.add).then_inc(lg_read, 1)

        def normalise(i):
            tiles = ds(i * BT, BT)
            dve.wait_ge(o_ready, i + 1)
            nc.vector.tensor_tensor(x_sb[:, tiles, :].rearrange("p t f -> p (t f)"),
                                    ps_w.rearrange("p b f -> p (b f)"),
                                    x_sb[:, tiles, :].rearrange("p t f -> p (t f)"), ALU.add).then_inc(residual, 1)
            wait_apart(dve, count, residual, i + 1, half_set, 1)
            for t in range(BT):
                last = nc.vector.bn_stats(stats[:, t, :], x_sb[:, ds(i * BT + t, 1), :].squeeze(1))
            last.then_inc(stat_step, 1)
            wait_apart(dve, count, stat_step, 2 * i + 1, half_set, 1)
            for t in range(BT):
                last = nc.vector.bn_aggr(mv[:, t, :], stats[:, t, :])
            last.then_inc(stat_step, 1)
            dve.wait_ge(stat_step, 2 * i + 2)
            nc.vector.tensor_scalar_add(var[:], mv[:, :, 1], LN_EPS).then_inc(var_ready, 1)
            if not at_start(i) and not (isinstance(i, int) and i == 1):
                read_logits(i - 2)
            dve.wait_ge(rstd_ready, i + 1)
            if not at_start(i):
                dve.wait_ge(t_ready, i)
            for t in range(BT):
                last = nc.vector.tensor_scalar(xn[:, t, :], x_sb[:, ds(i * BT + t, 1), :].squeeze(1),
                                               mv[:, t, 0:1], rstd[:, t:t + 1], ALU.subtract, ALU.mult)
            last.then_inc(xn_ready, 1)

        def step(i):
            cols = ds(i * BLOCK, BLOCK)
            dve.wait_ge(hi_ready, i + 1)
            nc.vector.tensor_tensor(xT_lo[:, :, cols], ps_t, xT_hi[:, :, cols].bitcast(F32), ALU.subtract
                                    ).then_inc(lo_ready, 1)
            if not at_end(i, 1):
                normalise(i + 1)

        normalise(0)
        steps(dve, step, 1)
        for i in range(BLOCKS - 2, BLOCKS):
            read_logits(i)

    @block.tensor
    def _(pe):
        def heads(i):
            pe.wait_ge(band_in, 16 * (i + 1))
            pe.wait_ge(staged, i + 1)
            for m in range(KD):
                if not at_start(i):
                    pe.wait_ge(a_copied[m], i)
                feats = slice(m * P, (m + 1) * P)
                for t in range(BT):
                    nc.tensor.matmul(ps_a[m][:, t * P:(t + 1) * P], o_st[:, t, feats], jump[:],
                                     start=t == 0, stop=False)
                for t in range(BT):
                    q0, q1 = max(0, t * P - WINDOW), min(BLOCK, (t + 1) * P + WINDOW)
                    c0 = t * WIN + q0 - (t * P - WINDOW)
                    nc.tensor.matmul(ps_a[m][:, q0:q1], v_st[:, t, feats], band[:, c0:c0 + q1 - q0],
                                     start=False, stop=False)
                for q0, c0 in ((0, BT * WIN), (BLOCK - WINDOW, BT * WIN + WINDOW)):
                    last = nc.tensor.matmul(ps_a[m][:, q0:q0 + WINDOW], v_halo[:, feats], band[:, c0:c0 + WINDOW],
                                            start=False, stop=q0 > 0)
                last.then_inc(a_ready[m], 1)

        def projection(i):
            for m in range(KD):
                pe.wait_ge(a_copied[m], i + 1)
            if not at_start(i):
                pe.wait_ge(residual, i)
            for t in range(BT):
                for k in range(KD):
                    last = nc.tensor.matmul(ps_w[:, t // 2, (t % 2) * DIM:(t % 2 + 1) * DIM],
                                            attnT[:, k, t * P:(t + 1) * P], w_o[:, k, :],
                                            start=k == 0, stop=k == KD - 1)
            last.then_inc(o_ready, 1)

        def transposes(i):
            pe.wait_ge(xn_ready, i + 1)
            if not at_start(i):
                pe.wait_ge(lo_ready, i)
            for k in range(KD):
                for t in range(BT):
                    last = nc.tensor.transpose(ps_t[:, k, t * P:(t + 1) * P], xn[:, t, k * P:(k + 1) * P], ident[:])
            last.then_inc(t_ready, 1)

        def router(i):
            pe.wait_ge(lo_ready, i + 1)
            cols = ds(i * BLOCK, BLOCK)
            for m in range(MR):
                if m == 0 and not at_start(i):
                    pe.wait_ge(lg_copied, i)
                elif m == 1 and not at_start(i):
                    pe.wait_ge(lg_read, i)
                elif m > 1:
                    pe.wait_ge(rh_ready[m - 2], i + 1)
                feats = slice(m * P, (m + 1) * P)
                terms = [(w, xs, k) for w, xs in ((w_r1_hi, xT_hi), (w_r1_hi, xT_lo), (w_r1_lo, xT_hi))
                         for k in range(KD)]
                for n, (w, xs, k) in enumerate(terms):
                    last = nc.tensor.matmul(ps_r[m % 2], w[:, k, feats], xs[:, k, cols],
                                            start=n == 0, stop=n == len(terms) - 1)
                last.then_inc(r_ready[m], 1)

        def router_logits(i):
            for m in range(MR):
                pe.wait_ge(rh_ready[m], i + 1)
            for m in range(MR):
                last = nc.tensor.matmul(ps_r[0][m * QUAD:(m + 1) * QUAD, :], w_r2[:, m, :], rh[:, m, :],
                                        start=True, stop=True)
            last.then_inc(lg_ready, 1)

        def transpose_logits(i):
            pe.wait_ge(lg_copied, i + 1)
            for c in range(BT):
                last = nc.tensor.transpose(ps_r[1][:, c * P:(c + 1) * P], logitsT[:, c * P:(c + 1) * P], ident[:])
            last.then_inc(lg_tr, 1)

        def step(i):
            transposes(i)
            if not at_start(i):
                router_logits(i - 1)
            if not at_end(i, 1):
                projection(i + 1)
            if not at_start(i):
                transpose_logits(i - 1)
            if not at_end(i, 2):
                heads(i + 2)
            router(i)

        heads(0)
        projection(0)
        heads(1)
        steps(pe, step, 2)
        router_logits(BLOCKS - 1)
        transpose_logits(BLOCKS - 1)


def experts(nc, ctx, dram, keep):
    def sb(name, shape, dt=F32):
        return ctx.enter_context(nc.sbuf_tensor(name, shape, dt))

    def sem(name):
        return ctx.enter_context(nc.semaphore(name))

    LAG, PS_H, H, HALVES, Y = 2, 4, 2, 4, 2
    x_sb, xT_hi, xT_lo, logits = (keep[n] for n in ("x", "xT_hi", "xT_lo", "logits"))
    raw1 = sb("raw1", [P, KD, HIDDEN])
    raw2 = sb("raw2", [P, MH, DIM])
    w1 = [(sb(f"w1_hi{u}", [P, KD, HIDDEN], F32R), sb(f"w1_lo{u}", [P, KD, HIDDEN], F32R)) for u in range(2)]
    w2 = [(sb(f"w2_hi{u}", [P, MH, DIM], F32R), sb(f"w2_lo{u}", [P, MH, DIM], F32R)) for u in range(2)]
    b1 = sb("b1", [P, EXPERTS, MH])
    b2 = sb("b2", [P, EXPERTS, DIM])
    b_r2 = sb("b_r2", [P, EXPERTS])
    before = sb("before", [P, 2, EXPERTS, EXPERTS])
    h = [sb(f"h{c}", [P, BLOCK]) for c in range(H)]
    h_hi = [sb(f"h_hi{c}", [P, BLOCK], F32R) for c in range(HALVES)]
    h_lo = [sb(f"h_lo{c}", [P, BLOCK], F32R) for c in range(HALVES)]
    top = sb("top", [P, TILES])
    prob = sb("prob", [P, TILES, EXPERTS])
    beaten = sb("beaten", [P, TILES, EXPERTS, EXPERTS])
    level = sb("level", [P, TILES, EXPERTS, EXPERTS])
    rank = sb("rank", [P, TILES, EXPERTS])
    gate = sb("gate", [P, TILES, EXPERTS])
    psum = ctx.enter_context(nc.psum_tensor("psum_experts", [P, 8, BLOCK], F32))
    ps_h = [psum[:, c, :] for c in range(PS_H)]
    ps_y = [[psum[:, PS_H + 2 * u + t // 2, (t % 2) * DIM:(t % 2 + 1) * DIM] for t in range(BT)] for u in range(Y)]

    CUT1, CUT2 = 4, 2
    cols = [slice(c * HIDDEN // CUT1, (c + 1) * HIDDEN // CUT1) for c in range(CUT1)]
    rows = [slice(c * MH // CUT2, (c + 1) * MH // CUT2) for c in range(CUT2)]
    parts = ([(raw1[:, :, s], w1[0][0][:, :, s], w1[0][1][:, :, s]) for s in cols] +
             [(raw2[:, s, :], w2[0][0][:, s, :], w2[0][1][:, s, :]) for s in rows])
    const_in = sem("expert_const_in")
    logits_in = sem("logits_consts_in")
    part_in = [sem(f"part_in{c}") for c in range(CUT1 + CUT2)]
    part_hi, part_lo = sem("part_hi"), sem("part_lo")
    raw_in, hi_set, lo_set = sem("raw_in"), sem("weights_hi"), sem("weights_lo")
    gate_step, shifted, exp_ready = sem("gate_step"), sem("shifted"), sem("exp_ready")
    h_ready = sem("h_ready")
    gelu_done = sem("gelu_done")
    hi_ready = sem("h_hi_ready")
    lo_ready = sem("h_lo_ready")
    h_used = sem("h_used")
    y_ready = sem("y_ready")
    y_read = sem("y_read")
    acc_done, out_stored = sem("acc_done"), sem("out_stored")
    pairs = BLOCKS // 2

    block = ctx.enter_context(nc.Block())

    @block.sync
    def _(sp):
        def all_partitions(name, pattern):
            return dram[name].rearrange(pattern, o=1).partition_broadcast(P)

        we1 = [dram["We1"][e].rearrange("(k p) n -> p k n", p=P) for e in range(EXPERTS)]
        we2 = [dram["We2"][e].rearrange("(k p) n -> p k n", p=P) for e in range(EXPERTS)]
        for c, s in enumerate(cols):
            sp.dma_start(raw1[:, :, s], we1[0][:, :, s]).then_inc(part_in[c], 16)
            if c == 0:
                sp.dma_start(b_r2[:], all_partitions("rb2", "(o e) -> o e")).then_inc(logits_in, 16)
                sp.dma_start(b1[:], dram["be1"]).then_inc(const_in, 16)
        sp.dma_start(before[:], all_partitions("before", "(o c) e j -> o c e j")).then_inc(const_in, 16)
        for c, s in enumerate(rows):
            sp.dma_start(raw2[:, s, :], we2[0][:, s, :]).then_inc(part_in[CUT1 + c], 16)
        sp.dma_start(b2[:], all_partitions("be2", "(o e) f -> o e f")).then_inc(const_in, 16)
        for e in range(1, EXPERTS):
            if e == 1:
                sp.wait_ge(part_lo, CUT1 + CUT2)
            else:
                sp.wait_ge(lo_set, 2 * (e - 1))
            sp.dma_start(raw1[:], we1[e]).then_inc(raw_in, 16)
            sp.dma_start(raw2[:], we2[e]).then_inc(raw_in, 16)
        with sp.Fori(0, BLOCKS) as b:
            sp.wait_ge(acc_done, (EXPERTS - 1) * BLOCKS + b + 1)
            sp.dma_start(dram["out"].rearrange("(n p) f -> p n f", p=P)[:, ds(b * BT, BT), :],
                         x_sb[:, ds(b * BT, BT), :]).then_inc(out_stored, 16)
        sp.wait_ge(out_stored, 16 * BLOCKS)

    @block.gpsimd
    def _(pool):
        for e in range(1, EXPERTS):
            pool.wait_ge(raw_in, 32 * e)
            if e >= 2:
                pool.wait_ge(h_used, MH * BLOCKS * (e - 1) + HALVES)
            for n, (raw, w) in enumerate(((raw1, w1), (raw2, w2))):
                nc.gpsimd.tensor_copy(w[e % 2][0][:], raw[:]).then_inc(hi_set, 1)
                pool.wait_ge(hi_set, 2 * (e - 1) + n + 1)
                nc.gpsimd.tensor_tensor(w[e % 2][1][:], raw[:], w[e % 2][0][:].bitcast(F32), ALU.subtract
                                        ).then_inc(lo_set, 1)
                pool.wait_ge(lo_set, 2 * (e - 1) + n + 1)

    @block.scalar
    def _(act):
        act.sem_inc(lo_ready, H)

        def hi(c):
            raw, w_hi, w_lo = parts[c]
            act.wait_ge(part_in[c], 16)
            nc.scalar.activation(w_hi, raw, ACT.Copy).then_inc(part_hi, 1)

        for c in range(CUT1):
            hi(c)
        act.wait_ge(shifted, 1)
        nc.scalar.activation(prob[:], prob[:], ACT.Exp).then_inc(exp_ready, 1)
        for c in range(CUT1, CUT1 + CUT2):
            hi(c)
        act.wait_ge(const_in, 16 * 3)
        for e in range(EXPERTS):
            with act.Fori(0, BLOCKS) as b:
                for m in range(MH):
                    s = MH * (e * BLOCKS + b) + m
                    act.wait_ge(lo_ready, s + 1)
                    act.wait_ge(h_ready, s + 1)
                    nc.scalar.activation(h[m % H][:], ps_h[m % PS_H], ACT.Gelu, bias=b1[:, e, m:m + 1]
                                         ).then_inc(gelu_done, 1)

    @block.vector
    def _(dve):
        done = [0]

        def gate_op(instruction):
            instruction.then_inc(gate_step, 1)
            done[0] += 1
            dve.wait_ge(gate_step, done[0])

        def lo(c):
            raw, w_hi, w_lo = parts[c]
            dve.wait_ge(part_hi, c + 1)
            nc.vector.tensor_tensor(w_lo, raw, w_hi.bitcast(F32), ALU.subtract).then_inc(part_lo, 1)

        dve.sem_inc(h_used, HALVES)
        per_tile = [P, TILES, EXPERTS]
        versus = [P, TILES, EXPERTS, EXPERTS]
        dve.wait_ge(logits_in, 16)
        gate_op(nc.vector.tensor_tensor(logits[:], logits[:], b_r2[:].unsqueeze(1).broadcast_to(per_tile), ALU.add))
        gate_op(nc.vector.tensor_reduce(top[:], logits[:], axis=AXIS.X, op=ALU.max))
        nc.vector.tensor_tensor(prob[:], logits[:], top[:].unsqueeze(2).broadcast_to(per_tile), ALU.subtract
                                ).then_inc(shifted, 1)
        for c in range(CUT1 + CUT2):
            lo(c)

        def halves(n, m):
            s = MH * n + m
            dve.wait_ge(h_used, s + 1)
            dve.wait_ge(gelu_done, s + 1 + PS_H)
            nc.vector.tensor_copy(h_hi[m % HALVES][:], h[m % H][:]).then_inc(hi_ready, 1)
            dve.wait_ge(hi_ready, s + 1)
            nc.vector.tensor_tensor(h_lo[m % HALVES][:], h[m % H][:], h_hi[m % HALVES][:].bitcast(F32),
                                    ALU.subtract).then_inc(lo_ready, 1)

        def accumulate(e, b, u):
            n = e * BLOCKS + b
            if e > 0:
                dve.wait_ge(acc_done, n - BLOCKS + 1)
            for t in range(BT):
                acc, g = x_sb[:, ds(b * BT + t, 1), :].squeeze(1), gate[:, ds(b * BT + t, 1), e]
                if t == 0:
                    dve.wait_ge(y_ready, n + 1)
                elif t == 2:
                    dve.wait_ge(h_used, MH * (n + 1) + HALVES)
                nc.vector.scalar_tensor_tensor(acc, ps_y[u][t], g, acc, ALU.mult, ALU.add).then_inc(y_read, 1)
            for t in range(BT):
                acc, g = x_sb[:, ds(b * BT + t, 1), :].squeeze(1), gate[:, ds(b * BT + t, 1), e]
                dve.wait_ge(y_read, BT * n + t + 1 + BT * Y)
                last = nc.vector.scalar_tensor_tensor(acc, b2[:, e, :], g, acc, ALU.mult, ALU.add)
            last.then_inc(acc_done, 1)

        for m in range(LAG):
            halves(0, m)
        dve.wait_ge(const_in, 16 * 3)
        dve.wait_ge(exp_ready, 1)
        gate_op(nc.vector.tensor_reduce(top[:], prob[:], axis=AXIS.X, op=ALU.add))
        gate_op(nc.vector.reciprocal(top[:], top[:]))
        gate_op(nc.vector.tensor_tensor(prob[:], prob[:], top[:].unsqueeze(2).broadcast_to(per_tile), ALU.mult))
        p_j, p_e = prob[:].unsqueeze(2).broadcast_to(versus), prob[:].unsqueeze(3).broadcast_to(versus)
        for c, (scratch, op) in enumerate(((beaten[:], ALU.is_gt), (level[:], ALU.is_ge))):
            gate_op(nc.vector.tensor_tensor(scratch, p_j, p_e, op))
            gate_op(nc.vector.tensor_tensor(scratch, scratch, before[:, c].unsqueeze(1).broadcast_to(versus),
                                            ALU.mult))
        gate_op(nc.vector.tensor_tensor(beaten[:], beaten[:], level[:], ALU.add))
        gate_op(nc.vector.tensor_reduce(rank[:], beaten[:], axis=AXIS.X, op=ALU.add))
        gate_op(nc.vector.tensor_scalar(rank[:], rank[:], 1.5, None, ALU.is_lt))
        gate_op(nc.vector.tensor_tensor(gate[:], prob[:], rank[:], ALU.mult))
        for e in range(EXPERTS):
            def body(i, last):
                for u in range(2):
                    b = 2 * i + u
                    n = e * BLOCKS + b
                    for m in range(LAG, MH):
                        halves(n, m)
                    if not (last and u and e == EXPERTS - 1):
                        for m in range(LAG):
                            halves(n + 1, m)
                    accumulate(e, b, u)

            twice(dve, pairs, body)

    @block.tensor
    def _(pe):
        pe.sem_inc(gelu_done, PS_H)
        pe.sem_inc(y_read, BT * Y)

        def hidden(e, b, m):
            s = MH * (e * BLOCKS + b) + m
            pe.wait_ge(gelu_done, s + 1)
            feats, toks = slice(m * P, (m + 1) * P), ds(b * BLOCK, BLOCK)
            hi, lo = w1[e % 2]
            terms = [(w, xs, k) for w, xs in ((hi, xT_hi), (hi, xT_lo), (lo, xT_hi)) for k in range(KD)]
            for j, (w, xs, k) in enumerate(terms):
                last = nc.tensor.matmul(ps_h[m % PS_H], w[:, k, feats], xs[:, k, toks],
                                        start=j == 0, stop=j == len(terms) - 1)
            last.then_inc(h_ready, 1)

        def output(e, b, u, m):
            n = e * BLOCKS + b
            hi, lo = w2[e % 2]
            pe.wait_ge(lo_ready, MH * n + m + 1 + H)
            if m == 0:
                pe.wait_ge(y_read, BT * (n + 1))
            for t in range(BT):
                toks = slice(t * P, (t + 1) * P)
                for j, (hs, w) in enumerate(((h_hi, hi), (h_hi, lo), (h_lo, hi))):
                    last = nc.tensor.matmul(ps_y[u][t], hs[m % HALVES][:, toks], w[:, m, :],
                                            start=m == 0 and j == 0 and t % 2 == 0,
                                            stop=m == MH - 1 and j == 2 and t % 2 == 1)
                if t == BT - 1:
                    last.then_inc(h_used, 1)
                elif t == 1 and m == MH - 1:
                    last.then_inc(y_ready, 1)

        for m in range(LAG):
            pe.wait_ge(part_lo, m * P // (HIDDEN // CUT1) + 1)
            hidden(0, 0, m)
        pe.wait_ge(part_lo, CUT1 + CUT2)
        for e in range(EXPERTS):
            def body(i, last):
                for u in range(2):
                    b = 2 * i + u
                    ends = last and u == 1
                    for m in range(MH):
                        if m < MH - LAG:
                            hidden(e, b, m + LAG)
                        elif not ends:
                            hidden(e, b + 1, m + LAG - MH)
                        elif e < EXPERTS - 1:
                            if m == MH - LAG:
                                pe.wait_ge(lo_set, 2 * (e + 1))
                            hidden(e + 1, 0, m + LAG - MH)
                        output(e, b, u, m)

            twice(pe, pairs, body)


def program(nc, dram):
    with ExitStack() as whole:
        def sb(name, shape, dt=F32):
            return whole.enter_context(nc.sbuf_tensor(name, shape, dt))

        keep = {
            "x": sb("x_sb", [P, TILES, DIM]), "ident": sb("ident_sb", [P, P]), "jump": sb("jump_sb", [P, P]),
            "ident16": sb("ident16", [P, P], BF16), "logits": sb("logits", [P, TILES, EXPERTS]),
        }
        dram["qk_pieces"] = nc.dram_tensor("qk_pieces", (2, NHEADS, HD, PIECES, SEQ), BF16, kind="Internal").ap()
        with ExitStack() as tokens:
            keep["v"] = tokens.enter_context(nc.sbuf_tensor("v_sb", [P, NHEADS, ST + 2, HD], F32))
            keep["o"] = tokens.enter_context(nc.sbuf_tensor("o_sb", [P, NHEADS + 1, ST, HD], F32))
            keep["w_o"] = tokens.enter_context(nc.sbuf_tensor("w_o", [P, KD, DIM], F32))
            for n in ("w_r1_hi", "w_r1_lo"):
                keep[n] = tokens.enter_context(nc.sbuf_tensor(n, [P, KD, RHID], F32R))
            keep["w_r2"] = tokens.enter_context(nc.sbuf_tensor("w_r2", [P, MR, QUAD], F32))
            keep["b_r1"] = tokens.enter_context(nc.sbuf_tensor("b_r1", [P, MR], F32))
            with ExitStack() as heads:
                for n in ("max_q0", "max_k0"):
                    keep[n] = heads.enter_context(nc.sbuf_tensor(n, [STACK, SEQ], BF16))
                keep["w_v"] = heads.enter_context(nc.sbuf_tensor("w_v", [P, KD, DIM], F32))
                keep["bias_v"] = heads.enter_context(nc.sbuf_tensor("bias_v", [P, DIM], F32))
                keep["xnT"] = keep["o"][:, 1:NHEADS + 1].rearrange("p (b k h) t d -> p b k (h t d)", b=BLOCKS, k=KD)
                for stage in (project, attend):
                    with ExitStack() as ctx:
                        stage(nc, ctx, dram, keep)
            for n in ("xT_hi", "xT_lo"):
                keep[n] = whole.enter_context(nc.sbuf_tensor(n, [P, KD, TOKENS], F32R, side="right"))
            with ExitStack() as ctx:
                route(nc, ctx, dram, keep)
        with ExitStack() as ctx:
            experts(nc, ctx, dram, keep)


def local_band():
    q, t = np.arange(SEQ)[:, None], np.arange(SEQ)[None, :]
    d = (q - t).astype(np.float32)
    k = np.where(np.abs(d) <= WINDOW, np.exp(-d ** 2 / np.float32(2.0 * LOCAL_STRENGTH ** 2)), np.float32(0))
    k = k / (k.sum(-1, keepdims=True, dtype=np.float32) + np.float32(EPS))
    k = (np.float32(1.0 - JUMP) * k).astype(np.float32)
    padded = np.zeros((SEQ + 2 * P, SEQ + 2 * P), np.float32)
    padded[P:-P, P:-P] = k
    band = np.zeros((BPS, P, BAND), np.float32)
    for j in range(BPS):
        start = P + j * BLOCK
        for t in range(BT):
            key = start + t * P
            band[j, :, t * WIN:(t + 1) * WIN] = padded[key - WINDOW:key + P + WINDOW, key:key + P].T
        halo = band[j, :, BT * WIN:]
        halo[96:, 0:WINDOW] = padded[start:start + WINDOW, start - P:start].T[96:]
        end = start + BLOCK
        halo[:96, WINDOW:] = padded[end - WINDOW:end, end:end + P].T[:96]
    return band


def kernel(**inputs):
    import concourse.bacc as bacc
    from concourse.bass_utils import run_bass_kernel_spmd

    a = {n.split("_", 2)[2]: np.asarray(v) for n, v in inputs.items() if n.startswith("L0_attn_")}
    f = {n.split("_", 2)[2]: np.asarray(v) for n, v in inputs.items() if n.startswith("L0_ffn_")}
    eye = np.eye(P, dtype=np.float32)
    j, e = np.arange(EXPERTS)[None, :], np.arange(EXPERTS)[:, None]
    w_r2 = np.zeros((RHID, QUAD), np.float32)
    w_r2[:, :EXPERTS] = f["rW2"]

    def columns(v):
        return v.reshape(-1, P).T

    arrays = {
        "x": a["x"].reshape(TOKENS, DIM),
        "wqT": a["Wq"].T, "wkT": a["Wk"].T, "wvT": a["Wv"].T, "woT": a["Wo"].T,
        "bq": columns(a["bq"]), "bk": columns(a["bk"]), "bv": a["bv"], "bo": a["bo"],
        "rW1": f["rW1"], "rb1": columns(f["rb1"]), "rW2": w_r2, "rb2": f["rb2"],
        "We1": f["We1"], "be1": f["be1"].reshape(EXPERTS, MH, P).transpose(2, 0, 1), "We2": f["We2"], "be2": f["be2"],
        "ident": eye, "jump": np.float32(JUMP) * eye, "band": local_band(),
        "before": np.stack([j > e, j < e]).astype(np.float32),
    }
    nc = bacc.Bacc("TRN2", target_bir_lowering=False, num_devices=1)
    arrays = {n: np.ascontiguousarray(v) for n, v in arrays.items()}
    dram = {n: nc.dram_tensor(f"in_{n}", v.shape, mybir.dt.from_np(v.dtype), kind="ExternalInput").ap()
            for n, v in arrays.items()}
    dram["out"] = nc.dram_tensor("out", (TOKENS, DIM), F32, kind="ExternalOutput").ap()
    program(nc, dram)
    r = run_bass_kernel_spmd(nc, [{f"in_{n}": v for n, v in arrays.items()}], core_ids=[0])
    return r.results[0]["out"].reshape(BATCH, SEQ, DIM)
```
